# Optimizing a Trainium2 kernel written in Bass

```python
import numpy as np
import jax
import jax.numpy as jnp

def _softmax(x, axis=-1):
    return jax.nn.softmax(x, axis=axis)
def _gelu(x):
    return jax.nn.gelu(x, approximate=True)
def _silu(x):
    return jax.nn.silu(x)
def _sigmoid(x):
    return jax.nn.sigmoid(x)
def _layernorm(x, axis=-1, eps=1e-5):
    m = jnp.mean(x, axis=axis, keepdims=True)
    v = jnp.var(x, axis=axis, keepdims=True)
    return (x - m) / jnp.sqrt(v + eps)
def _scatter_add(tgt, idx, src, axis=0):
    return tgt.at[idx].add(src)
def _segment_sum(src, seg, n):
    return jax.ops.segment_sum(src, seg, n)

kernel_name = 'mk_conv_preact_d4_conv_nchw32_7b67e4'

def setup_inputs(seed: int = 0):
    np.random.seed(seed)
    _w = jnp.asarray
    def _rec_inputs():
        import jax
        import jax.numpy as jnp
        _gk = jax.random.key(seed)
        x = -0.0001329 + 0.9999 * jax.random.normal(jax.random.fold_in(_gk, 1), (8, 32, 384, 384), jnp.float32)
        return x
    x = _rec_inputs()
    def _L0_conv_setup():
        import jax, jax.numpy as jnp
        import numpy as np
        from jax import lax
        B, C, H, W = (16, 32, 384, 384)
        NK = 32
        K = 3
        HID = 128
        key = jax.random.key(seed)
        ks = jax.random.split(key, 5)
        x = jax.random.normal(ks[0], (B, C, H, W), dtype=jnp.float32)
        w1 = jax.random.normal(ks[1], (C, HID), dtype=jnp.float32) * (1.0 / np.sqrt(C))
        b1 = jnp.zeros((HID,), dtype=jnp.float32)
        w2 = jax.random.normal(ks[2], (HID, NK * K * K), dtype=jnp.float32) * (1.0 / np.sqrt(HID))
        b2 = jnp.zeros((NK * K * K,), dtype=jnp.float32)
        return {'x': x, 'w1': w1, 'b1': b1, 'w2': w2, 'b2': b2}
    _L0_conv_all = _L0_conv_setup()
    _L0_conv_in = {k: v for k, v in _L0_conv_all.items() if k in ('w1', 'b1', 'w2', 'b2', )}
    del _L0_conv_all

    def _L1_conv_setup():
        import jax, jax.numpy as jnp
        import numpy as np
        from jax import lax

        def ste_sign(t):
            return t + lax.stop_gradient(jnp.sign(t) - t)
        key = jax.random.key(seed)
        kx, kw = jax.random.split(key)
        x = jax.random.normal(kx, (8, 32, 384, 384), dtype=jnp.float32)
        W = jax.random.normal(kw, (32, 32, 3, 3), dtype=jnp.float32)
        return {'x': x, 'W': W}
    _L1_conv_all = _L1_conv_setup()
    _L1_conv_in = {k: v for k, v in _L1_conv_all.items() if k in ('W', )}
    del _L1_conv_all

    def _L2_conv_setup():
        import jax, jax.numpy as jnp
        import numpy as np
        from jax import lax
        B, C, H, W = (16, 32, 384, 384)
        NK = 32
        K = 3
        HID = 128
        key = jax.random.key(seed)
        ks = jax.random.split(key, 5)
        x = jax.random.normal(ks[0], (B, C, H, W), dtype=jnp.float32)
        w1 = jax.random.normal(ks[1], (C, HID), dtype=jnp.float32) * (1.0 / np.sqrt(C))
        b1 = jnp.zeros((HID,), dtype=jnp.float32)
        w2 = jax.random.normal(ks[2], (HID, NK * K * K), dtype=jnp.float32) * (1.0 / np.sqrt(HID))
        b2 = jnp.zeros((NK * K * K,), dtype=jnp.float32)
        return {'x': x, 'w1': w1, 'b1': b1, 'w2': w2, 'b2': b2}
    _L2_conv_all = _L2_conv_setup()
    _L2_conv_in = {k: v for k, v in _L2_conv_all.items() if k in ('w1', 'b1', 'w2', 'b2', )}
    del _L2_conv_all

    def _L3_conv_setup():
        import jax, jax.numpy as jnp
        import numpy as np
        from jax import lax
        B, C, H, W = (16, 32, 384, 384)
        NK = 32
        K = 3
        HID = 128
        key = jax.random.key(seed)
        ks = jax.random.split(key, 5)
        x = jax.random.normal(ks[0], (B, C, H, W), dtype=jnp.float32)
        w1 = jax.random.normal(ks[1], (C, HID), dtype=jnp.float32) * (1.0 / np.sqrt(C))
        b1 = jnp.zeros((HID,), dtype=jnp.float32)
        w2 = jax.random.normal(ks[2], (HID, NK * K * K), dtype=jnp.float32) * (1.0 / np.sqrt(HID))
        b2 = jnp.zeros((NK * K * K,), dtype=jnp.float32)
        return {'x': x, 'w1': w1, 'b1': b1, 'w2': w2, 'b2': b2}
    _L3_conv_all = _L3_conv_setup()
    _L3_conv_in = {k: v for k, v in _L3_conv_all.items() if k in ('w1', 'b1', 'w2', 'b2', )}
    del _L3_conv_all

    return {
        "x": x,
        "L0_conv_w1": _L0_conv_in["w1"],
        "L0_conv_b1": _L0_conv_in["b1"],
        "L0_conv_w2": _L0_conv_in["w2"],
        "L0_conv_b2": _L0_conv_in["b2"],
        "L1_conv_W": _L1_conv_in["W"],
        "L2_conv_w1": _L2_conv_in["w1"],
        "L2_conv_b1": _L2_conv_in["b1"],
        "L2_conv_w2": _L2_conv_in["w2"],
        "L2_conv_b2": _L2_conv_in["b2"],
        "L3_conv_w1": _L3_conv_in["w1"],
        "L3_conv_b1": _L3_conv_in["b1"],
        "L3_conv_w2": _L3_conv_in["w2"],
        "L3_conv_b2": _L3_conv_in["b2"],
    }

def reference(x, L0_conv_w1, L0_conv_b1, L0_conv_w2, L0_conv_b2, L1_conv_W, L2_conv_w1, L2_conv_b1, L2_conv_w2, L2_conv_b2, L3_conv_w1, L3_conv_b1, L3_conv_w2, L3_conv_b2):
    import jax
    import jax.numpy as jnp
    def _L0_conv_ref(x, w1, b1, w2, b2):
        import jax, jax.numpy as jnp
        import numpy as np
        from jax import lax
        B, C, H, W = (16, 32, 384, 384)
        NK = 32
        K = 3
        HID = 128
        b, c, h, w = x.shape
        pooled = x.mean(axis=(2, 3))
        hdn = jax.nn.relu(pooled @ w1 + b1)
        kernels = (hdn @ w2 + b2).reshape(b, NK, K, K)
        xg = x[:, :NK].reshape(1, b * NK, h, w)
        wgt = kernels.reshape(b * NK, 1, K, K)
        pad = K // 2
        out = lax.conv_general_dilated(xg, wgt, window_strides=(1, 1), padding=[(pad, pad), (pad, pad)], feature_group_count=b * NK, dimension_numbers=('NCHW', 'OIHW', 'NCHW'))
        return out.reshape(b, NK, h, w)

    def _L1_conv_ref(x, W):
        import jax, jax.numpy as jnp
        import numpy as np
        from jax import lax

        def ste_sign(t):
            return t + lax.stop_gradient(jnp.sign(t) - t)
        xb = ste_sign(x)
        wb = ste_sign(W)
        out = lax.conv_general_dilated(xb, wb, window_strides=(1, 1), padding=[(1, 1), (1, 1)], dimension_numbers=('NCHW', 'OIHW', 'NCHW'))
        return out

    def _L2_conv_ref(x, w1, b1, w2, b2):
        import jax, jax.numpy as jnp
        import numpy as np
        from jax import lax
        B, C, H, W = (16, 32, 384, 384)
        NK = 32
        K = 3
        HID = 128
        b, c, h, w = x.shape
        pooled = x.mean(axis=(2, 3))
        hdn = jax.nn.relu(pooled @ w1 + b1)
        kernels = (hdn @ w2 + b2).reshape(b, NK, K, K)
        xg = x[:, :NK].reshape(1, b * NK, h, w)
        wgt = kernels.reshape(b * NK, 1, K, K)
        pad = K // 2
        out = lax.conv_general_dilated(xg, wgt, window_strides=(1, 1), padding=[(pad, pad), (pad, pad)], feature_group_count=b * NK, dimension_numbers=('NCHW', 'OIHW', 'NCHW'))
        return out.reshape(b, NK, h, w)

    def _L3_conv_ref(x, w1, b1, w2, b2):
        import jax, jax.numpy as jnp
        import numpy as np
        from jax import lax
        B, C, H, W = (16, 32, 384, 384)
        NK = 32
        K = 3
        HID = 128
        b, c, h, w = x.shape
        pooled = x.mean(axis=(2, 3))
        hdn = jax.nn.relu(pooled @ w1 + b1)
        kernels = (hdn @ w2 + b2).reshape(b, NK, K, K)
        xg = x[:, :NK].reshape(1, b * NK, h, w)
        wgt = kernels.reshape(b * NK, 1, K, K)
        pad = K // 2
        out = lax.conv_general_dilated(xg, wgt, window_strides=(1, 1), padding=[(pad, pad), (pad, pad)], feature_group_count=b * NK, dimension_numbers=('NCHW', 'OIHW', 'NCHW'))
        return out.reshape(b, NK, h, w)

    def _gn(v, G=16, eps=1e-5):
        B_, C_, H_, W_ = v.shape
        g = v.reshape(B_, G, C_ // G, H_, W_)
        m = jnp.mean(g, axis=(2, 3, 4), keepdims=True)
        s = jnp.var(g, axis=(2, 3, 4), keepdims=True)
        return ((g - m) / jnp.sqrt(s + eps)).reshape(v.shape)

    def _ln_c(v, eps=1e-6):
        m = jnp.mean(v, axis=1, keepdims=True)
        s = jnp.var(v, axis=1, keepdims=True)
        return (v - m) / jnp.sqrt(s + eps)

    def _ln_t(v, eps=1e-5):
        m = jnp.mean(v, axis=-1, keepdims=True)
        s = jnp.var(v, axis=-1, keepdims=True)
        return (v - m) / jnp.sqrt(s + eps)

    def _to_tokens(v):
        B_, C_, H_, W_ = v.shape
        return v.reshape(B_, C_, H_ * W_).transpose(0, 2, 1)
    def _from_tokens(t, like):
        B_, C_, H_, W_ = like.shape
        return t.transpose(0, 2, 1).reshape(B_, C_, H_, W_)

    x = x + _L0_conv_ref(_gn(x), L0_conv_w1, L0_conv_b1, L0_conv_w2, L0_conv_b2)
    x = x + _L1_conv_ref(_gn(x), L1_conv_W)
    x = x + _L2_conv_ref(_gn(x), L2_conv_w1, L2_conv_b1, L2_conv_w2, L2_conv_b2)
    x = x + _L3_conv_ref(_gn(x), L3_conv_w1, L3_conv_b1, L3_conv_w2, L3_conv_b2)
    return x


_drawn_inputs = setup_inputs


def setup_inputs(seed=0):
    import zlib

    import numpy as np

    out = dict(_drawn_inputs(seed))
    spreads = {'L0_conv_b1': (0.0, 0.1),
     'L0_conv_b2': (0.0, 0.1),
     'L2_conv_b1': (0.0, 0.736),
     'L2_conv_b2': (0.0, 0.497),
     'L3_conv_b1': (0.0, 0.712),
     'L3_conv_b2': (0.0, 0.469)}
    factors = {'L2_conv_w1': 64.0, 'L2_conv_w2': 4.727, 'L3_conv_w1': 64.0, 'L3_conv_w2': 4.706}
    for name, (base, spread) in spreads.items():
        noise = np.random.default_rng([zlib.crc32(name.encode()), seed]).standard_normal(out[name].shape)
        drawn = base * np.exp(spread * noise) if base else spread * noise
        out[name] = jnp.asarray(drawn.astype(out[name].dtype))
    for name, factor in factors.items():
        out[name] = (out[name] * factor).astype(out[name].dtype)
    return out
```

```python
from contextlib import ExitStack

import numpy as np

import concourse.bass as bass
from concourse import mybir
from concourse.alu_op_type import AluOpType as ALU

ACT = mybir.ActivationFunctionType
AX = mybir.AxisListType
F32 = mybir.dt.float32
F16 = mybir.dt.float16

B, C, H, W = 8, 32, 384, 384
HID = 128
TAPS = 9
R = 8
CH = 16
P = R * CH
HV = C // CH
G = H // R
DG = 2
DUOS = G // DG
SLOTS = 4
TURNS = DUOS // SLOTS
RG = SLOTS * DG
WP = W + 2
LAYERS = 4
DENSE = 1
DEPTHWISE = [0, 2, 3]
GN_EPS = 1e-5
X_SCALE = 64.0
W_SCALE = 1024.0
EVAC_LAG = 3
STORE_LAG = 4
LOAD_LAG = 5
STAT_LAG = 6


def shape_constants():
    p = np.arange(P)
    row, ch = p // CH, p % CH
    r_out = np.arange(R)
    pair = ((ch[:, None] // 2) == (ch[None, :] // 2)).astype(np.float32) / (2 * R)
    same = (ch[:, None] == np.arange(CH)[None, :]).astype(np.float32)
    dy = np.arange(3) - 1
    main = (row[:, None, None] == r_out[None, None, :] + dy[None, :, None]).astype(np.float32)
    def edge(before):
        m = np.zeros((P, 3, R), np.float32)
        m[before, 0, 0] = 1.0
        m[~before, 2, R - 1] = 1.0
        return m
    halo = edge((p // CH) % 2 == 0)
    halo_dense = edge((p // C) % 2 == 0)
    return np.concatenate([pair, same, main.reshape(P, -1), halo.reshape(P, -1), halo_dense.reshape(P, -1)],
                          axis=1).astype(np.float32)


C_SAME = P
C_MAIN = C_SAME + CH
C_HALO = C_MAIN + 3 * R
C_HALO_DENSE = C_HALO + 3 * R
C_ALL = C_HALO_DENSE + 3 * R


def halo_copies(layer, slot):
    places = 4 if layer == DENSE else 3
    return places * (3 if slot in (0, SLOTS - 1) else 2)


def halo_value(s, layer, turns, slot):
    sample = sum(TURNS * halo_copies(l, slot) for l in range(LAYERS))
    before = sum(TURNS * halo_copies(l, slot) for l in range(layer))
    return (s * sample + turns * halo_copies(layer, slot) + before + 1) * 16


class Step:

    def __init__(self, j, k, i):
        self.j, self.k, self.i = j, k, i

    def lagged(self, lag):
        if self.i is not None and not 0 <= self.i - lag < DUOS:
            return None
        return self.j + (self.k - lag) // SLOTS, (self.k - lag) % SLOTS


def steps(eng, lag):
    peeled = -(-lag // SLOTS)
    for i in range(peeled * SLOTS):
        yield Step(i // SLOTS, i % SLOTS, i)
    with eng.Fori(peeled, TURNS) as j:
        for k in range(SLOTS):
            yield Step(j, k, None)
    for i in range(DUOS, DUOS + lag):
        yield Step(i // SLOTS, i % SLOTS, i)


def for_samples(eng, body):
    with eng.Fori(0, B - 1) as s:
        body(s, False)
    body(B - 1, True)


def conv_preact_kernel(nc, x, w1, b1, w2, b2, w_dense, consts, out):
    ctx = ExitStack()
    with ctx:
        def sb(name, shape, dt):
            return ctx.enter_context(nc.sbuf_tensor(name, shape, dt))

        def sem(name):
            return ctx.enter_context(nc.semaphore(name))

        y = sb("y", [P, HV, G, W], F32)
        ring = sb("ring", [P, 2, HV, RG, WP], F16)
        halo = sb("halo", [P, SLOTS, HV, DG, WP], F16)
        zero_row = sb("zero_row", [CH, HV, WP], F16)
        xn = sb("xn", [P, HV, DG * W], F32)
        w_main = sb("w_main", [P, HV, 2, 3, P], F16)
        w_halo = sb("w_halo", [P, HV, 3, P], F16)
        wd_main = sb("wd_main", [P, HV, HV, 3, P], F16)
        wd_halo = sb("wd_halo", [P, HV, 2, P], F16)
        cst = sb("cst", [P, C_ALL], F32)
        w1_sb = sb("w1_sb", [P, 3, HV, HID], F32)
        w2_sb = sb("w2_sb", [HID, 3, C * TAPS], F32)
        b1_sb = sb("b1_sb", [HID, 3], F32)
        b2_sb = sb("b2_sb", [P, 3, HV, TAPS], F32)
        stats = sb("stats", [P, HV, G, 6], F32)
        agg = sb("agg", [P, HV, 2], F32)
        dev = sb("dev", [P, HV], F32)
        spread = sb("spread", [P, HV], F32)
        var = sb("var", [P, HV], F32)
        std = sb("std", [P, HV], F32)
        rstd = sb("rstd", [P, HV], F32)
        newton = sb("newton", [P, HV], F32)
        x_mul = sb("x_mul", [P, HV], F32)
        x_add = sb("x_add", [P, HV], F32)
        neg_mean = sb("neg_mean", [P, HV], F32)
        pooled = sb("pooled", [P, HV], F32)
        hidden = sb("hidden", [HID, P], F32)
        taps = sb("taps", [P, HV, TAPS], F32)
        tap_max = sb("tap_max", [P, HV], F32)
        tap_inv = sb("tap_inv", [P, HV], F32)
        out_mul = sb("out_mul", [P, HV], F32)
        parts = sb("parts", [P, HV, 2, 3, 3], F16)
        rows = sb("rows", [P, 2 * HV * 3, R], F32)
        acc = ctx.enter_context(nc.psum_tensor("acc", [P, 2, HV, DG, 512], F32))

        dense_raw = xn[:, 0, 0:C * TAPS]
        stage = xn[:, 1, 0:C * TAPS]
        ps_mean = acc[:, 0, 0, 0, 0:HV]
        ps_var = acc[:, 0, 0, 1, 0:HV]
        ps_hidden = acc[:, 0, 1, 0, 0:1]
        ps_taps = acc[:, 0, 1, 1, 0:C * TAPS]
        picked = acc[:, 1, 0, 0, 0:C * TAPS].rearrange("p (v c t) -> p v c t", v=HV, t=TAPS)
        rows_t = acc[:, 1, 0, 1, 0:2 * HV * 3 * R].rearrange("p (n r) -> p n r", r=R)

        pair_avg = cst[:, 0:P]
        same_ch = cst[:, C_SAME:C_MAIN]
        main_rows = cst[:, C_MAIN:C_HALO].rearrange("p (d r) -> p d r", d=3)
        halo_rows = cst[:, C_HALO:C_HALO_DENSE].rearrange("p (d r) -> p d r", d=3)
        halo_rows_dense = cst[:, C_HALO_DENSE:C_ALL].rearrange("p (d r) -> p d r", d=3)

        params_in = sem("params_in")
        dense_in = [sem(f"dense_in{n}") for n in range(3)]
        stage_free = sem("stage_free")
        cleared = sem("cleared")
        setup_chain = sem("setup_chain")
        dense_ready = sem("dense_ready")
        duo_stats = sem("duo_stats")
        chain = sem("chain")
        loaded = [sem(f"loaded{k}") for k in range(SLOTS)]
        stored = [sem(f"stored{k}") for k in range(SLOTS)]
        agg_ready = sem("agg_ready")
        mean_ready = sem("mean_ready")
        spread_ready = sem("spread_ready")
        group_var_ready = sem("group_var_ready")
        var_ready = sem("var_ready")
        std_ready = sem("std_ready")
        affine_ready = sem("affine_ready")
        pooled_ready = sem("pooled_ready")
        hidden_sum_ready = sem("hidden_sum_ready")
        hidden_ready = sem("hidden_ready")
        taps_ready = sem("taps_ready")
        weights_ready = sem("weights_ready")
        xn_ready = sem("xn_ready")
        high_ready = [sem(f"high_ready{h}") for h in range(HV)]
        low_ready = [sem(f"low_ready{h}") for h in range(HV)]
        halo_copied = [sem(f"halo_copied{k}") for k in range(SLOTS)]
        acc_full = [[sem(f"acc_full{k}{h}") for h in range(HV)] for k in range(SLOTS)]
        ring_released = [acc_full[k][HV - 1] for k in range(SLOTS)]
        acc_free = [[sem(f"acc_free{q}{h}") for h in range(HV)] for q in range(2)]

        wait_carrier = sem("wait_carrier")

        def settle(eng):
            eng.sem_inc(wait_carrier, 1)

        credited = [*(x for pair in acc_full + acc_free for x in pair), *low_ready]

        def duo_count(s, layer, j, k):
            return s * (LAYERS * DUOS) + j * SLOTS + (layer * DUOS + k)

        def split_count(s, layer, j, k):
            return s * (len(DEPTHWISE) * DUOS) + j * SLOTS + (DEPTHWISE.index(layer) * DUOS + k + 1)

        def slot_uses(s, layer, j):
            return s * (LAYERS * TURNS) + j + (layer * TURNS + 1)

        def acc_uses(s, layer, j, k):
            return s * (LAYERS * DUOS // 2) + j * (SLOTS // 2) + (layer * DUOS // 2 + k // 2 + 1)

        def duo_rows(j, k):
            g0 = j * RG + k * DG
            return y[:, :, bass.ds(g0, DG), :]

        block = ctx.enter_context(nc.Block())

        @block.sync
        def _(sp):
            def load(s, j, k):
                sp.dma_start(duo_rows(j, k), x[s, :, :, bass.ds(j * RG + k * DG, DG), :]).then_inc(loaded[k], 16)

            for i in range(SLOTS):
                load(0, 0, i)
            sp.dma_start(cst[:], consts).then_inc(params_in, 16)
            for r in range(R):
                sp.dma_start(dense_raw[r * CH:(r + 1) * CH, :], w_dense[0:CH, :]).then_inc(dense_in[0], 16)
            for n in range(3):
                for r in range(R):
                    sp.dma_start(w1_sb[r * CH:(r + 1) * CH, n], w1[n].rearrange("(v c) m -> c v m", v=HV))\
                        .then_inc(params_in, 16)
                    sp.dma_start(b2_sb[r * CH:(r + 1) * CH, n],
                                 b2[n].rearrange("(v c t) -> c v t", v=HV, t=TAPS)).then_inc(params_in, 16)
                sp.dma_start(w2_sb[:, n, :], w2[n]).then_inc(params_in, 16)
                sp.dma_start(b1_sb[:, n:n + 1], b1[n].rearrange("(m a) -> m a", a=1)).then_inc(params_in, 16)
            with sp.Fori(1, TURNS) as j:
                for k in range(SLOTS):
                    sp.wait_ge(loaded[k], j * 16)
                    load(0, j, k)
            for n in (1, 2):
                sp.wait_ge(stage_free, n)
                if n == 1:
                    for r in range(R):
                        sp.dma_start(dense_raw[r * CH:(r + 1) * CH, :], w_dense[CH:C, :]).then_inc(dense_in[1], 16)
                else:
                    for q in range(P // C):
                        sp.dma_start(dense_raw[q * C:(q + 1) * C, :], w_dense[0:C, :]).then_inc(dense_in[2], 16)

            def copy_halo(s, layer, j, k):
                first = isinstance(j, int) and j == 0 and k == 0
                last = isinstance(j, int) and j == TURNS - 1 and k == SLOTS - 1
                sp.wait_ge(ring_released[k], slot_uses(s, layer, j))
                settle(sp)
                g0 = k * DG

                def spans(edge):
                    if edge == 0:
                        if k == 0:
                            return [(0, 1, None if first else RG - 1), (1, 1, 0)]
                        return [(0, DG, g0 - 1)]
                    if k == SLOTS - 1:
                        return [(0, 1, g0 + 1), (1, 1, None if last else 0)]
                    return [(0, DG, g0 + 1)]

                for edge in (0, 1):
                    r = R - 1 if edge == 0 else 0
                    for g, n, src in spans(edge):
                        for place in range(halo_copies(layer, 1) // 2):
                            if layer == DENSE:
                                shift, h = place // 2, place % 2
                                p0 = shift * 64 + edge * 32 + h * CH
                                cols = slice(shift, WP)
                                dst = halo[p0:p0 + CH, k, 0, g:g + n, 0:WP - shift]
                                if src is None:
                                    from_ = zero_row[:, 0:1, cols]
                                else:
                                    from_ = ring[r * CH:(r + 1) * CH, 0, h, src:src + n, cols]
                            else:
                                p0 = place * 32 + edge * CH
                                dst = halo[p0:p0 + CH, k, :, g:g + n, :]
                                if src is None:
                                    from_ = zero_row[:, :, :].rearrange("p v (g w) -> p v g w", g=1)
                                else:
                                    from_ = ring[r * CH:(r + 1) * CH, place % 2, :, src:src + n, :]
                            sp.dma_start(dst, from_).then_inc(halo_copied[k], 16)

            def sample(s, last):
                for layer in range(LAYERS):
                    final = layer == LAYERS - 1
                    lag = 1 if not final else STORE_LAG if last else LOAD_LAG
                    for step in steps(sp, lag):
                        made = step.lagged(0)
                        if made:
                            if layer == DENSE:
                                for h in range(HV):
                                    sp.wait_ge(high_ready[h], duo_count(s, layer, *made) + 1)
                                    settle(sp)
                            else:
                                for h in range(HV):
                                    sp.wait_ge(low_ready[h], split_count(s, layer, *made) + 1)
                                    settle(sp)
                        target = step.lagged(1)
                        if target:
                            copy_halo(s, layer, *target)
                        done = step.lagged(STORE_LAG) if final else None
                        if done:
                            j, k = done
                            for h in range(HV):
                                sp.wait_ge(acc_free[k % 2][h], acc_uses(s, layer, j, k) + 1)
                                settle(sp)
                            sp.dma_start(out[s, :, :, bass.ds(j * RG + k * DG, DG), :], duo_rows(j, k))\
                                .then_inc(stored[k], 16)
                        gone = step.lagged(LOAD_LAG) if final and not last else None
                        if gone:
                            j, k = gone
                            sp.wait_ge(stored[k], (s * TURNS + j + 1) * 16)
                            settle(sp)
                            sp.wait_ge(loaded[k], (s * TURNS + j + TURNS) * 16)
                            settle(sp)
                            load(s + 1, j, k)

            sp.wait_ge(cleared, 2)
            for_samples(sp, sample)
            for k in range(SLOTS):
                sp.wait_ge(stored[k], B * TURNS * 16)

        @block.gpsimd
        def _(pool):
            for start in credited:
                pool.sem_inc(start, 1)
            for start in halo_copied:
                pool.sem_inc(start, 16)
            pool.memset(ring[:].rearrange("p a v g w -> p (a v g w)").bitcast(F32), 0.0).then_inc(cleared, 1)
            pool.memset(zero_row[:].rearrange("p v w -> p (v w)").bitcast(F32), 0.0).then_inc(cleared, 1)

        @block.scalar
        def _(act):
            act.wait_ge(cleared, 2)
            act.wait_ge(dense_ready, 1)

            def sample(s, last):
                for layer in range(LAYERS):
                    if layer != DENSE:
                        act.wait_ge(var_ready, s * len(DEPTHWISE) + DEPTHWISE.index(layer) + 1)
                        nc.scalar.activation(std[:], var[:], ACT.Sqrt).then_inc(std_ready, 1)
                    act.wait_ge(affine_ready, s * LAYERS + layer + 1)
                    with act.Fori(0, TURNS) as j:
                        for k in range(SLOTS):
                            act.wait_ge(ring_released[k], slot_uses(s, layer, j))
                            k_next = (k + 1) % SLOTS
                            act.wait_ge(halo_copied[k_next],
                                        halo_value(s, layer, j + 1 if k == SLOTS - 1 else j, k_next)
                                        if k == SLOTS - 1 else halo_value(s, layer, j, k_next))
                            for h in range(HV):
                                src = y[:, h, bass.ds(j * RG + k * DG, DG), :]
                                dst = ring[:, 0, h, k * DG:(k + 1) * DG, 1:W + 1]
                                if layer == DENSE:
                                    nc.scalar.activation(dst, src, ACT.Sign, bias=neg_mean[:, h:h + 1])\
                                        .then_inc(high_ready[h], 1)
                                    continue
                                n = split_count(s, layer, j, k)
                                act.wait_ge(low_ready[h], n)
                                nc.scalar.activation(xn[:, h].rearrange("p (g w) -> p g w", g=DG), src, ACT.Identity,
                                                     bias=x_add[:, h:h + 1], scale=x_mul[:, h:h + 1])\
                                    .then_inc(xn_ready, 1)
                            if layer != DENSE:
                                for h in range(HV):
                                    dst = ring[:, 0, h, k * DG:(k + 1) * DG, 1:W + 1]
                                    act.wait_ge(xn_ready, (n - 1) * HV + h + 1)
                                    nc.scalar.copy(dst, xn[:, h].rearrange("p (g w) -> p g w", g=DG))\
                                        .then_inc(high_ready[h], 1)

            for_samples(act, sample)

        @block.vector
        def _(dve):
            count = [0]

            def setup(ins):
                count[0] += 1
                ins.then_inc(setup_chain, 1)
                dve.wait_ge(setup_chain, count[0])

            def expand(dst, by_row, n):
                return nc.vector.tensor_tensor(
                    dst.rearrange("p (n r c) -> p (n r) c", n=n, c=CH),
                    by_row.rearrange("p n r -> p (n r)").unsqueeze(2).to_broadcast([dst.shape[0], n * R, CH]),
                    same_ch[0:dst.shape[0]].unsqueeze(1).to_broadcast([dst.shape[0], n * R, CH]), ALU.mult)

            dve.wait_ge(params_in, 16 * (1 + 3 * (2 * R + 2)))
            setup(nc.vector.tensor_scalar(w1_sb[:], w1_sb[:], 1.0 / R, None, ALU.mult))

            for n in range(3):
                dve.wait_ge(dense_in[n], 16 * (R if n < 2 else P // C))
                setup(nc.vector.tensor_scalar(stage, dense_raw, 0.0, None, ALU.is_lt))
                setup(nc.vector.scalar_tensor_tensor(stage, dense_raw, 0.0, stage, ALU.is_gt, ALU.subtract))
                signs = stage.rearrange("p (o t) -> p o t", t=TAPS)
                row_mask = main_rows if n < 2 else halo_rows_dense
                for v in range(HV):
                    for dx in range(3):
                        if n < 2:
                            p0, p1, dst = 0, P, wd_main[:, v, n, dx, :]
                        elif dx == 1:
                            p0, p1, dst = 64, P, wd_halo[64:P, v, 0, :]
                        else:
                            p0, p1, dst = 0, 64, wd_halo[0:64, v, dx // 2, :]
                        view = dst.rearrange("p (r c) -> p r c", c=CH)
                        shape = [p1 - p0, R, CH]
                        part_sum = hidden[p0:p1, :].rearrange("p (r c) -> p r c", c=CH)
                        term = acc[p0:p1, 0, 0, 0, 0:P].rearrange("p (r c) -> p r c", c=CH)
                        for dy in range(3):
                            a = row_mask[p0:p1, dy, :].unsqueeze(2).to_broadcast(shape)
                            b = signs[p0:p1, v * CH:(v + 1) * CH, dy * 3 + dx].unsqueeze(1).to_broadcast(shape)
                            setup(nc.vector.tensor_tensor(part_sum if dy == 0 else term, a, b, ALU.mult))
                            if dy:
                                setup(nc.vector.tensor_tensor(view if dy == 2 else part_sum, part_sum, term, ALU.add))
                if n < 2:
                    dve.sem_inc(stage_free, 1)
            dve.sem_inc(dense_ready, 1)

            def row_stats(j, k):
                for h in range(HV):
                    for g in range(DG):
                        at = j * RG + (k * DG + g)
                        ins = nc.vector.bn_stats(stats[:, h, bass.ds(at, 1), :].rearrange("p a b -> p (a b)"),
                                                 y[:, h, bass.ds(at, 1), :].rearrange("p a b -> p (a b)"))
                ins.then_inc(duo_stats, 1)

            with dve.Fori(0, TURNS) as j:
                for k in range(SLOTS):
                    dve.wait_ge(loaded[k], (j + 1) * 16)
                    row_stats(j, k)

            def sample(s, last):
                done = [0]

                def link(ins):
                    done[0] += 1
                    ins.then_inc(chain, 1)
                    dve.wait_ge(chain, s * CHAIN + done[0])

                for layer in range(LAYERS):
                    n_layer = s * LAYERS + layer + 1
                    dve.wait_ge(duo_stats, n_layer * DUOS)
                    settle(dve)
                    for h in range(HV):
                        last_agg = nc.vector.bn_aggr(agg[:, h, :], stats[:, h].rearrange("p g s -> p (g s)"))
                    last_agg.then_inc(agg_ready, 1)
                    dve.wait_ge(mean_ready, n_layer)
                    if layer == DENSE:
                        nc.vector.tensor_scalar(neg_mean[:], ps_mean, -1.0, None, ALU.mult).then_inc(affine_ready, 1)
                    else:
                        n_split = s * len(DEPTHWISE) + DEPTHWISE.index(layer) + 1
                        w_at = DEPTHWISE.index(layer)
                        link(nc.vector.tensor_tensor(dev[:], agg[:, :, 0], ps_mean, ALU.subtract))
                        link(nc.vector.tensor_tensor(spread[:], dev[:], dev[:], ALU.mult))
                        nc.vector.tensor_tensor(spread[:], spread[:], agg[:, :, 1], ALU.add).then_inc(spread_ready, 1)
                        dve.wait_ge(group_var_ready, n_split)
                        nc.vector.tensor_scalar(var[:], ps_var, GN_EPS, None, ALU.add).then_inc(var_ready, 1)
                        dve.wait_ge(std_ready, n_split)
                        link(nc.vector.reciprocal(rstd[:], std[:]))
                        link(nc.vector.tensor_tensor(newton[:], rstd[:], rstd[:], ALU.mult))
                        link(nc.vector.tensor_tensor(newton[:], newton[:], var[:], ALU.mult))
                        link(nc.vector.tensor_scalar(newton[:], newton[:], -0.5, 1.5, ALU.mult, ALU.add))
                        link(nc.vector.tensor_tensor(rstd[:], rstd[:], newton[:], ALU.mult))
                        nc.vector.tensor_tensor(pooled[:], dev[:], rstd[:], ALU.mult).then_inc(pooled_ready, 1)
                        link(nc.vector.tensor_scalar(x_mul[:], rstd[:], X_SCALE, None, ALU.mult))
                        nc.vector.scalar_tensor_tensor(x_add[:], ps_mean, -1.0, x_mul[:], ALU.mult, ALU.mult)\
                            .then_inc(affine_ready, 1)
                        dve.wait_ge(hidden_sum_ready, n_split)
                        nc.vector.tensor_scalar(hidden[:], ps_hidden.to_broadcast([HID, P]),
                                                b1_sb[:, w_at:w_at + 1], 0.0, ALU.add, ALU.max).then_inc(hidden_ready, 1)
                        dve.wait_ge(taps_ready, n_split)
                        for h in range(HV):
                            pick = nc.vector.tensor_tensor(
                                picked[:, h], ps_taps.rearrange("p (v c t) -> p v c t", v=HV, t=TAPS)[:, h],
                                same_ch.unsqueeze(2).to_broadcast([P, CH, TAPS]), ALU.mult)
                        link(pick)
                        link(nc.vector.tensor_reduce(taps[:], picked.rearrange("p v c t -> p v t c"), AX.X, ALU.add))
                        link(nc.vector.tensor_tensor(taps[:], taps[:], b2_sb[:, w_at], ALU.add))
                        link(nc.vector.tensor_reduce(tap_max[:], taps[:], AX.X, ALU.max, apply_absolute_value=True))
                        link(nc.vector.tensor_scalar(tap_max[:], tap_max[:], 1e-30, None, ALU.max))
                        nc.vector.tensor_scalar(out_mul[:], tap_max[:], 1.0 / (W_SCALE * X_SCALE), None, ALU.mult)
                        link(nc.vector.reciprocal(tap_inv[:], tap_max[:]))
                        for h in range(HV):
                            scaled = nc.vector.tensor_scalar(taps[:, h], taps[:, h], tap_inv[:, h:h + 1], W_SCALE,
                                                             ALU.mult, ALU.mult)
                        link(scaled)
                        flat = parts[:].rearrange("p v a y x -> p v a (y x)")
                        link(nc.vector.tensor_copy(flat[:, :, 0], taps[:]))
                        link(nc.vector.tensor_tensor(flat[:, :, 1], taps[:], flat[:, :, 0], ALU.subtract))
                        shape = [P, 2 * HV, 3, R]
                        by = parts[:].rearrange("p v a y x -> p (v a) y x")
                        rows_v = rows[:].rearrange("p (n x) r -> p n x r", x=3)
                        rows_tv = rows_t.rearrange("p (n x) r -> p n x r", x=3)
                        for dy in range(3):
                            link(nc.vector.tensor_tensor(rows_v if dy == 0 else rows_tv,
                                                         by[:, :, dy, :].unsqueeze(3).to_broadcast(shape),
                                                         main_rows[:, dy, :].unsqueeze(1).unsqueeze(1).to_broadcast(shape),
                                                         ALU.mult))
                            if dy:
                                link(nc.vector.tensor_tensor(rows[:], rows[:], rows_t, ALU.add))
                        link(expand(w_main[:].rearrange("p v a x m -> p (v a x m)"), rows[:], 2 * HV * 3))
                        for p0, p1, a in ((0, 64, 0), (64, 96, 1)):
                            shape = [p1 - p0, HV, 3, R]
                            rows_v = rows[p0:p1, 0:HV * 3].rearrange("p (n x) r -> p n x r", x=3)
                            rows_tv = rows_t[p0:p1, 0:HV * 3].rearrange("p (n x) r -> p n x r", x=3)
                            for dy in (0, 2):
                                link(nc.vector.tensor_tensor(
                                    rows_v if dy == 0 else rows_tv,
                                    parts[p0:p1, :, a, dy, :].unsqueeze(3).to_broadcast(shape),
                                    halo_rows[p0:p1, dy, :].unsqueeze(1).unsqueeze(1).to_broadcast(shape), ALU.mult))
                            link(nc.vector.tensor_tensor(rows_v, rows_v, rows_tv, ALU.add))
                        expand(w_halo[0:96].rearrange("p v x m -> p (v x m)"), rows[0:96, 0:HV * 3], HV * 3)\
                            .then_inc(weights_ready, 1)

                    final = layer == LAYERS - 1
                    for step in steps(dve, EVAC_LAG if not final or last else STAT_LAG):
                        split = step.lagged(0) if layer != DENSE else None
                        if split:
                            j, k = split
                            for h in range(HV):
                                dve.wait_ge(high_ready[h], duo_count(s, layer, j, k) + 1)
                                spot = ring[:, :, h, k * DG:(k + 1) * DG, 1:W + 1]
                                nc.vector.tensor_tensor(spot[:, 1], xn[:, h].rearrange("p (g w) -> p g w", g=DG),
                                                        spot[:, 0], ALU.subtract).then_inc(low_ready[h], 1)
                        add = step.lagged(EVAC_LAG)
                        if add:
                            j, k = add
                            uses = acc_uses(s, layer, j, k)
                            for h in range(HV):
                                dve.wait_ge(acc_full[k][h], slot_uses(s, layer, j) + 1)
                                dst = y[:, h, bass.ds(j * RG + k * DG, DG), :]
                                src = acc[:, k % 2, h, :, 0:W]
                                if layer == DENSE:
                                    ins = nc.vector.tensor_tensor(dst, src, dst, ALU.add)
                                else:
                                    ins = nc.vector.scalar_tensor_tensor(dst, src, out_mul[:, h:h + 1], dst,
                                                                         ALU.mult, ALU.add)
                                ins.then_inc(acc_free[k % 2][h], 1)
                            if not final:
                                for h in range(HV):
                                    dve.wait_ge(acc_free[k % 2][h], uses + 1)
                                row_stats(j, k)
                        arrived = step.lagged(STAT_LAG) if final and not last else None
                        if arrived:
                            j, k = arrived
                            dve.wait_ge(loaded[k], (s * TURNS + j + TURNS + 1) * 16)
                            row_stats(j, k)
                assert done[0] == CHAIN, done

            for_samples(dve, sample)

        @block.tensor
        def _(pe):
            pe.wait_ge(params_in, 16 * (1 + 3 * (2 * R + 2)))
            pe.wait_ge(setup_chain, 1)
            pe.wait_ge(dense_ready, 1)

            def small(out_, lhsT, rhs, start=True, stop=True):
                return nc.tensor.matmul(out_, lhsT, rhs, start=start, stop=stop)

            def sample(s, last):
                for layer in range(LAYERS):
                    n_layer = s * LAYERS + layer + 1
                    pe.wait_ge(agg_ready, n_layer)
                    small(ps_mean, pair_avg, agg[:, :, 0]).then_inc(mean_ready, 1)
                    if layer != DENSE:
                        w_at = DEPTHWISE.index(layer)
                        n_split = s * len(DEPTHWISE) + w_at + 1
                        pe.wait_ge(spread_ready, n_split)
                        small(ps_var, pair_avg, spread[:]).then_inc(group_var_ready, 1)
                        pe.wait_ge(pooled_ready, n_split)
                        for h in range(HV):
                            hid = small(ps_hidden, w1_sb[:, w_at, h, :], pooled[:, h:h + 1], h == 0, h == HV - 1)
                        hid.then_inc(hidden_sum_ready, 1)
                        pe.wait_ge(hidden_ready, n_split)
                        small(ps_taps, hidden[:], w2_sb[:, w_at, :]).then_inc(taps_ready, 1)
                        pe.wait_ge(weights_ready, n_split)
                        settle(pe)
                    else:
                        pe.wait_ge(affine_ready, n_layer)
                        settle(pe)
                    with pe.Fori(0, TURNS) as j:
                        for k in range(SLOTS):
                            uses = acc_uses(s, layer, j, k)

                            def product(h, w, p1, src, n, total):
                                for g in range(DG):
                                    mm = nc.tensor.matmul(acc[:, k % 2, h, g, 0:W], w, src[:, g], start=(n == 0),
                                                          stop=(n == total - 1))
                                return mm

                            if layer == DENSE:
                                for h in range(HV):
                                    pe.wait_ge(high_ready[h], duo_count(s, layer, j, k) + 1)
                                total = HV * 3 + 2
                                for h in range(HV):
                                    pe.wait_ge(acc_free[k % 2][h], uses)
                                    for v in range(HV):
                                        for dx in range(3):
                                            product(h, wd_main[:, h, v, dx, :], P,
                                                    ring[:, 0, v, k * DG:(k + 1) * DG, dx:dx + W], v * 3 + dx, total)
                                pe.wait_ge(halo_copied[k], halo_value(s, layer, j + 1, k))
                                for h in range(HV):
                                    product(h, wd_halo[:, h, 0, :], P, halo[:, k, 0, :, 0:W], total - 2, total)
                                    full = product(h, wd_halo[0:64, h, 1, :], 64, halo[0:64, k, 0, :, 2:2 + W],
                                                   total - 1, total)
                                    full.then_inc(acc_full[k][h], 1)
                            else:
                                total = 3 * 3 + 3
                                for h in range(HV):
                                    pe.wait_ge(low_ready[h], split_count(s, layer, j, k) + 1)
                                    pe.wait_ge(acc_free[k % 2][h], uses)
                                    n = 0
                                    for a_w, a_x in ((0, 0), (0, 1), (1, 0)):
                                        for dx in range(3):
                                            product(h, w_main[:, h, a_w, dx, :], P,
                                                    ring[:, a_x, h, k * DG:(k + 1) * DG, dx:dx + W], n, total)
                                            n += 1
                                pe.wait_ge(halo_copied[k], halo_value(s, layer, j + 1, k))
                                for h in range(HV):
                                    for dx in range(3):
                                        full = product(h, w_halo[0:96, h, dx, :], 96, halo[0:96, k, h, :, dx:dx + W],
                                                       9 + dx, total)
                                    full.then_inc(acc_full[k][h], 1)
            for_samples(pe, sample)


CHAIN = 87


def kernel(**inputs):
    import concourse.bacc as bacc
    from concourse.bass_utils import run_bass_kernel_spmd

    def lay(a):
        return np.ascontiguousarray(a)

    xs = np.asarray(inputs["x"]).reshape(B, HV, CH, G, R, W).transpose(0, 4, 2, 1, 3, 5)
    arrays = {"x": lay(xs).reshape(B, P, HV, G, W)}
    for n, name in enumerate(("L0", "L2", "L3")):
        for part in ("w1", "b1", "w2", "b2"):
            arrays[f"{part}_{n}"] = lay(inputs[f"{name}_conv_{part}"])
    arrays["w_dense"] = lay(np.asarray(inputs["L1_conv_W"]).reshape(C, C, TAPS).transpose(1, 0, 2)).reshape(C, C * TAPS)
    arrays["consts"] = shape_constants()

    nc = bacc.Bacc("TRN2", target_bir_lowering=False, num_devices=1)
    aps = {name: nc.dram_tensor(name, a.shape, mybir.dt.from_np(a.dtype), kind="ExternalInput").ap()
           for name, a in arrays.items()}
    out = nc.dram_tensor("out", (B, P, HV, G, W), F32, kind="ExternalOutput").ap()
    conv_preact_kernel(nc, aps["x"], *([aps[f"{part}_{n}"] for n in range(3)] for part in ("w1", "b1", "w2", "b2")),
                       aps["w_dense"], aps["consts"], out)
    r = run_bass_kernel_spmd(nc, [arrays], core_ids=[0])
    got = r.results[0]["out"].reshape(B, R, CH, HV, G, W).transpose(0, 3, 2, 4, 1, 5)
    return lay(got).reshape(B, C, H, W)
```

```python
from contextlib import ExitStack

import numpy as np

import concourse.bass as bass
from concourse import mybir
from concourse.alu_op_type import AluOpType as ALU

ACT = mybir.ActivationFunctionType
AX = mybir.AxisListType
F32 = mybir.dt.float32
F16 = mybir.dt.float16

B, C, H, W = 8, 32, 384, 384
HID = 128
TAPS = 9
S = 2
R = 4
CH = 16
P = S * CH * R
HV = C // CH
G = H // R
WS = W // S
DG = 4
BG = 2
BANKS = DG // BG
NB = BG * WS
DUOS = G // DG
SLOTS = 4
HALO_SLOTS = 2
TURNS = DUOS // SLOTS
RG = SLOTS * DG
WP = WS + 2
LAYERS = 4
DENSE = 1
DEPTHWISE = [0, 2, 3]
GN_EPS = 1e-5
X_SCALE = 64.0
W_SCALE = 1024.0
EVAC_LAG = 3
STORE_LAG = 4
LOAD_LAG = 5
STAT_LAG = 6


CENTER, SIDES, EDGES = range(3)


def shape_constants():
    p = np.arange(P)
    parity, ch, row = p // (CH * R), p // R % CH, p % R
    pair = ((ch[:, None] // 2) == (ch[None, :] // 2)).astype(np.float32) / (2 * R * S)
    same = (ch[:, None] == np.arange(CH)[None, :]).astype(np.float32)
    use = np.zeros((P, 3, S, R, 3, 3), np.float32)
    for q in p:
        for s_out in range(S):
            for r_out in range(R):
                def enter(kind, y, x):
                    dy, dx = y - r_out, x - s_out
                    if abs(dy) <= 1 and abs(dx) <= 1:
                        use[q, kind, s_out, r_out, dy + 1, dx + 1] = 1.0
                enter(CENTER, row[q], parity[q])
                if s_out != parity[q]:
                    enter(SIDES, row[q], -1 if parity[q] else S)
                y = -1 if row[q] % 2 == 0 else R
                if row[q] < 2:
                    enter(EDGES, y, parity[q])
                elif s_out != parity[q]:
                    enter(EDGES, y, -1 if parity[q] else S)
    return np.concatenate([pair, same, use.reshape(P, -1)], axis=1).astype(np.float32)


C_SAME = P
C_USE = C_SAME + CH
C_ALL = C_USE + 3 * S * R * TAPS


def halo_copies(slot):
    return 9 if slot in (0, SLOTS - 1) else 6


HALO_TURN = halo_copies(0) + halo_copies(2)
assert HALO_TURN == halo_copies(1) + halo_copies(3)


def halo_value(s, layer, j, k):
    per_turn = HALO_TURN
    upto = sum(halo_copies(i) for i in range(k % HALO_SLOTS, k + 1, HALO_SLOTS))
    return (s * (LAYERS * TURNS * per_turn) + j * per_turn + (layer * TURNS * per_turn + upto + per_turn)) * 16


class Step:

    def __init__(self, j, k, i):
        self.j, self.k, self.i = j, k, i

    def lagged(self, lag):
        if self.i is not None and not 0 <= self.i - lag < DUOS:
            return None
        return self.j + (self.k - lag) // SLOTS, (self.k - lag) % SLOTS


def steps(eng, lag):
    peeled = -(-lag // SLOTS)
    for i in range(peeled * SLOTS):
        yield Step(i // SLOTS, i % SLOTS, i)
    with eng.Fori(peeled, TURNS) as j:
        for k in range(SLOTS):
            yield Step(j, k, None)
    for i in range(DUOS, DUOS + lag):
        yield Step(i // SLOTS, i % SLOTS, i)


def for_samples(eng, body):
    with eng.Fori(0, B - 1) as s:
        body(s, False)
    body(B - 1, True)


def conv_preact_kernel(nc, x, w1, b1, w2, b2, w_dense, consts, out):
    ctx = ExitStack()
    with ctx:
        def sb(name, shape, dt):
            return ctx.enter_context(nc.sbuf_tensor(name, shape, dt))

        def sem(name):
            return ctx.enter_context(nc.semaphore(name))

        y = sb("y", [P, HV, G, WS], F32)
        ring = sb("ring", [P, 2, HV, RG, WP], F16)
        halo = sb("halo", [P, HALO_SLOTS, 2, HV, DG, WP], F16)
        zero_row = sb("zero_row", [S * CH, 2, HV, WP], F16)
        xn = sb("xn", [P, HV, DG * WS], F32)
        w_split = sb("w_split", [P, HV, 2, 3, P], F16)
        w_signs = sb("w_signs", [P, HV, HV, 3, P], F16)
        cst = sb("cst", [P, C_ALL], F32)
        w1_sb = sb("w1_sb", [P, 3, HV, HID], F32)
        w2_sb = sb("w2_sb", [HID, 3, C * TAPS], F32)
        b1_sb = sb("b1_sb", [HID, 3], F32)
        b2_sb = sb("b2_sb", [P, 3, HV, TAPS], F32)
        stats = sb("stats", [P, HV, G // BG, 6], F32)
        agg = sb("agg", [P, HV, 2], F32)
        dev = sb("dev", [P, HV], F32)
        spread = sb("spread", [P, HV], F32)
        var = sb("var", [P, HV], F32)
        std = sb("std", [P, HV], F32)
        rstd = sb("rstd", [P, HV], F32)
        newton = sb("newton", [P, HV], F32)
        x_mul = sb("x_mul", [P, HV], F32)
        x_add = sb("x_add", [P, HV], F32)
        neg_mean = sb("neg_mean", [P, HV], F32)
        pooled = sb("pooled", [P, HV], F32)
        hidden = sb("hidden", [HID, P], F32)
        taps = sb("taps", [P, HV, TAPS], F32)
        tap_max = sb("tap_max", [P, HV], F32)
        tap_inv = sb("tap_inv", [P, HV], F32)
        out_mul = sb("out_mul", [P, HV], F32)
        parts = sb("parts", [P, HV, 2, TAPS], F16)
        by_place = sb("by_place", [P, HV, 2, 3 * S * R], F32)
        acc = ctx.enter_context(nc.psum_tensor("acc", [P, 2, HV, BANKS, 512], F32))

        dense_raw = xn[:, 0, 0:C * TAPS]
        stage = xn[:, 1, 0:C * TAPS]
        ps_mean = acc[:, 0, 0, 0, 0:HV]
        ps_var = acc[:, 0, 0, 1, 0:HV]
        ps_hidden = acc[:, 0, 1, 0, 0:1]
        ps_taps = acc[:, 0, 1, 1, 0:C * TAPS]
        picked = acc[:, 1, 0, 0, 0:C * TAPS].rearrange("p (v c t) -> p v c t", v=HV, t=TAPS)
        masked = [acc[:, 1, h, 1, 0:2 * 3 * S * R * TAPS].rearrange("p (a n t) -> p a n t", a=2, t=TAPS)
                  for h in range(HV)]

        pair_avg = cst[:, 0:P]
        same_ch = cst[:, C_SAME:C_USE]
        use = cst[:, C_USE:C_ALL].rearrange("p (k s n) -> p k s n", k=3, s=S)

        def replicas():
            for s in range(S):
                for r in range(R):
                    first = s * CH * R + r
                    yield slice(first, first + (CH - 1) * R + 1, R)

        params_in = sem("params_in")
        dense_in = [sem(f"dense_in{v}") for v in range(HV)]
        stage_free = sem("stage_free")
        cleared = sem("cleared")
        setup_chain = sem("setup_chain")
        dense_ready = sem("dense_ready")
        duo_stats = sem("duo_stats")
        chain = sem("chain")
        loaded = [sem(f"loaded{k}") for k in range(SLOTS)]
        stored = [sem(f"stored{k}") for k in range(SLOTS)]
        agg_ready = sem("agg_ready")
        mean_ready = sem("mean_ready")
        spread_ready = sem("spread_ready")
        group_var_ready = sem("group_var_ready")
        var_ready = sem("var_ready")
        std_ready = sem("std_ready")
        affine_ready = sem("affine_ready")
        pooled_ready = sem("pooled_ready")
        hidden_sum_ready = sem("hidden_sum_ready")
        hidden_ready = sem("hidden_ready")
        taps_ready = sem("taps_ready")
        weights_ready = sem("weights_ready")
        xn_ready = sem("xn_ready")
        high_ready = [sem(f"high_ready{h}") for h in range(HV)]
        low_ready = [sem(f"low_ready{h}") for h in range(HV)]
        halo_copied = [sem(f"halo_copied{k}") for k in range(HALO_SLOTS)]
        acc_full = [[sem(f"acc_full{k}{h}") for h in range(HV)] for k in range(SLOTS)]
        ring_released = [acc_full[k][HV - 1] for k in range(SLOTS)]
        acc_free = [[sem(f"acc_free{q}{h}") for h in range(HV)] for q in range(2)]

        wait_carrier = sem("wait_carrier")

        def settle(eng):
            eng.sem_inc(wait_carrier, 1)

        credited = [*(x for pair in acc_full + acc_free for x in pair), *low_ready]

        def duo_count(s, layer, j, k):
            return s * (LAYERS * DUOS) + j * SLOTS + (layer * DUOS + k)

        def split_count(s, layer, j, k):
            return s * (len(DEPTHWISE) * DUOS) + j * SLOTS + (DEPTHWISE.index(layer) * DUOS + k + 1)

        def slot_uses(s, layer, j):
            return s * (LAYERS * TURNS) + j + (layer * TURNS + 1)

        def acc_uses(s, layer, j, k):
            return s * (LAYERS * DUOS // 2) + j * (SLOTS // 2) + (layer * DUOS // 2 + k // 2 + 1)

        def duo_rows(j, k):
            return y[:, :, bass.ds(j * RG + k * DG, DG), :]

        block = ctx.enter_context(nc.Block())

        @block.sync
        def _(sp):
            def load(s, j, k):
                sp.dma_start(duo_rows(j, k), x[s, :, :, bass.ds(j * RG + k * DG, DG), :]).then_inc(loaded[k], 16)

            for i in range(SLOTS):
                load(0, 0, i)
            sp.dma_start(cst[:], consts).then_inc(params_in, 16)
            for at in replicas():
                sp.dma_start(dense_raw[at, :], w_dense[0:CH, :]).then_inc(dense_in[0], 16)
            for n in range(3):
                for at in replicas():
                    sp.dma_start(w1_sb[at, n], w1[n].rearrange("(v c) m -> c v m", v=HV)).then_inc(params_in, 16)
                    sp.dma_start(b2_sb[at, n], b2[n].rearrange("(v c t) -> c v t", v=HV, t=TAPS))\
                        .then_inc(params_in, 16)
                sp.dma_start(w2_sb[:, n, :], w2[n]).then_inc(params_in, 16)
                sp.dma_start(b1_sb[:, n:n + 1], b1[n].rearrange("(m a) -> m a", a=1)).then_inc(params_in, 16)
            with sp.Fori(1, TURNS) as j:
                for k in range(SLOTS):
                    sp.wait_ge(loaded[k], j * 16)
                    load(0, j, k)
            sp.wait_ge(stage_free, 1)
            for at in replicas():
                sp.dma_start(dense_raw[at, :], w_dense[CH:C, :]).then_inc(dense_in[1], 16)

            def copy_halo(s, layer, j, k):
                first = isinstance(j, int) and j == 0 and k == 0
                last = isinstance(j, int) and j == TURNS - 1 and k == SLOTS - 1
                before = (k - HALO_SLOTS) % SLOTS
                sp.wait_ge(ring_released[before], slot_uses(s, layer, j) + (0 if k < HALO_SLOTS else 1))
                settle(sp)
                tile = halo[:, k % HALO_SLOTS].rearrange("p a v g w -> p (a v) (g w)")
                held = ring[:].rearrange("p a v g w -> p (a v) (g w)")
                zeros = zero_row[:].rearrange("p a v w -> p (a v) w")
                nv = HV if layer == DENSE else 2 * HV
                g0 = k * DG

                for below in (0, 1):
                    if not below and k == 0:
                        spans = [(0, 1, None if first else RG - 1), (1, DG - 1, 0)]
                    elif not below:
                        spans = [(0, DG, g0 - 1)]
                    elif k == SLOTS - 1:
                        spans = [(0, DG - 1, g0 + 1), (DG - 1, 1, None if last else 0)]
                    else:
                        spans = [(0, DG, g0 + 1)]
                    row = 0 if below else R - 1
                    for part0, n, place, shift in ((0, S * CH, below, 0), (0, CH, 2 + below, -1), (CH, CH, 2 + below, 1)):
                        for g, ng, src in spans:
                            size = ng * WP - abs(shift)
                            at = slice(part0 * R + place, (part0 + n - 1) * R + place + 1, R)
                            from_at = slice(part0 * R + row, (part0 + n - 1) * R + row + 1, R)
                            d0, s0 = max(shift, 0), max(-shift, 0)
                            dst = tile[at, 0:nv, g * WP + d0:g * WP + d0 + size]
                            if src is None:
                                from_ = zeros[0:n, 0:nv, s0:s0 + size]
                            else:
                                from_ = held[from_at, 0:nv, src * WP + s0:src * WP + s0 + size]
                            sp.dma_start(dst, from_).then_inc(halo_copied[k % HALO_SLOTS], 16)

            def sample(s, last):
                for layer in range(LAYERS):
                    final = layer == LAYERS - 1
                    lag = 1 if not final else STORE_LAG if last else LOAD_LAG
                    for step in steps(sp, lag):
                        made = step.lagged(0)
                        if made:
                            if layer == DENSE:
                                for h in range(HV):
                                    sp.wait_ge(high_ready[h], duo_count(s, layer, *made) + 1)
                                    settle(sp)
                            else:
                                for h in range(HV):
                                    sp.wait_ge(low_ready[h], split_count(s, layer, *made) + 1)
                                    settle(sp)
                        target = step.lagged(1)
                        if target:
                            copy_halo(s, layer, *target)
                        done = step.lagged(STORE_LAG) if final else None
                        if done:
                            j, k = done
                            for h in range(HV):
                                sp.wait_ge(acc_free[k % 2][h], acc_uses(s, layer, j, k) + 1)
                                settle(sp)
                            sp.dma_start(out[s, :, :, bass.ds(j * RG + k * DG, DG), :], duo_rows(j, k))\
                                .then_inc(stored[k], 16)
                        gone = step.lagged(LOAD_LAG) if final and not last else None
                        if gone:
                            j, k = gone
                            sp.wait_ge(stored[k], (s * TURNS + j + 1) * 16)
                            settle(sp)
                            sp.wait_ge(loaded[k], (s * TURNS + j + TURNS) * 16)
                            settle(sp)
                            load(s + 1, j, k)

            sp.wait_ge(cleared, 2)
            for_samples(sp, sample)
            for k in range(SLOTS):
                sp.wait_ge(stored[k], B * TURNS * 16)

        @block.gpsimd
        def _(pool):
            for start in credited:
                pool.sem_inc(start, 1)
            for start in halo_copied:
                pool.sem_inc(start, 16 * HALO_TURN)
            pool.memset(ring[:].rearrange("p a v g w -> p (a v g w)").bitcast(F32), 0.0).then_inc(cleared, 1)
            pool.memset(zero_row[:].rearrange("p a v w -> p (a v w)").bitcast(F32), 0.0).then_inc(cleared, 1)

        @block.scalar
        def _(act):
            act.wait_ge(cleared, 2)
            act.wait_ge(dense_ready, 1)

            def sample(s, last):
                for layer in range(LAYERS):
                    if layer != DENSE:
                        act.wait_ge(var_ready, s * len(DEPTHWISE) + DEPTHWISE.index(layer) + 1)
                        nc.scalar.activation(std[:], var[:], ACT.Sqrt).then_inc(std_ready, 1)
                    act.wait_ge(affine_ready, s * LAYERS + layer + 1)
                    with act.Fori(0, TURNS) as j:
                        for k in range(SLOTS):
                            act.wait_ge(ring_released[k], slot_uses(s, layer, j))
                            act.wait_ge(halo_copied[(k + 1) % HALO_SLOTS],
                                        halo_value(s, layer, j, 0) if k == SLOTS - 1 else
                                        halo_value(s, layer, j - 1, k + 1))
                            for h in range(HV):
                                src = y[:, h, bass.ds(j * RG + k * DG, DG), :]
                                dst = ring[:, 0, h, k * DG:(k + 1) * DG, 1:WS + 1]
                                if layer == DENSE:
                                    nc.scalar.activation(dst, src, ACT.Sign, bias=neg_mean[:, h:h + 1])\
                                        .then_inc(high_ready[h], 1)
                                    continue
                                n = split_count(s, layer, j, k)
                                act.wait_ge(low_ready[h], n)
                                nc.scalar.activation(xn[:, h].rearrange("p (g w) -> p g w", g=DG), src, ACT.Identity,
                                                     bias=x_add[:, h:h + 1], scale=x_mul[:, h:h + 1])\
                                    .then_inc(xn_ready, 1)
                            if layer != DENSE:
                                for h in range(HV):
                                    dst = ring[:, 0, h, k * DG:(k + 1) * DG, 1:WS + 1]
                                    act.wait_ge(xn_ready, (n - 1) * HV + h + 1)
                                    nc.scalar.copy(dst, xn[:, h].rearrange("p (g w) -> p g w", g=DG))\
                                        .then_inc(high_ready[h], 1)

            for_samples(act, sample)

        @block.vector
        def _(dve):
            count = [0]

            def setup(ins):
                count[0] += 1
                ins.then_inc(setup_chain, 1)
                dve.wait_ge(setup_chain, count[0])

            dve.wait_ge(params_in, 16 * PARAM_DMAS)
            setup(nc.vector.tensor_scalar(w1_sb[:], w1_sb[:], 1.0 / (S * R), None, ALU.mult))

            signs = stage.rearrange("p (o t) -> p o t", t=TAPS)
            for v in range(HV):
                dve.wait_ge(dense_in[v], 16 * S * R)
                setup(nc.vector.tensor_scalar(stage, dense_raw, 0.0, None, ALU.is_lt))
                setup(nc.vector.scalar_tensor_tensor(stage, dense_raw, 0.0, stage, ALU.is_gt, ALU.subtract))
                if v == 0:
                    dve.sem_inc(stage_free, 1)
                for h in range(HV):
                    for kind in range(3):
                        for s_out in range(S):
                            for c0 in range(0, CH, CH // 2):
                                shape = [P, CH // 2, R, TAPS]
                                term = acc[:, 0, 0, (c0 > 0) * 1, 0:CH // 2 * R * TAPS]\
                                    .rearrange("p (c r t) -> p c r t", r=R, t=TAPS)
                                o = h * CH + c0
                                setup(nc.vector.tensor_tensor(
                                    term, signs[:, o:o + CH // 2, :].unsqueeze(2).to_broadcast(shape),
                                    use[:, kind, s_out, :].rearrange("p (r t) -> p r t", r=R).unsqueeze(1)
                                    .to_broadcast(shape), ALU.mult))
                                dst = w_signs[:, v, h, kind, :].rearrange("p (s c r) -> p s c r", s=S, r=R)
                                with nc.allow_low_precision(reason="one term of each sum is not zero"):
                                    nc.vector.tensor_reduce(dst[:, s_out, c0:c0 + CH // 2, :], term, AX.X, ALU.add)
            setup(nc.vector.memset(tap_max[:], 0.0))
            dve.sem_inc(dense_ready, 1)

            def row_stats(j, k):
                for h in range(HV):
                    for bank in range(BANKS):
                        ins = nc.vector.bn_stats(
                            stats[:, h, bass.ds(j * (SLOTS * BANKS) + (k * BANKS + bank), 1), :]
                            .rearrange("p a b -> p (a b)"),
                            y[:, h, bass.ds(j * RG + (k * DG + bank * BG), BG), :].rearrange("p a b -> p (a b)"))
                ins.then_inc(duo_stats, 1)

            with dve.Fori(0, TURNS) as j:
                for k in range(SLOTS):
                    dve.wait_ge(loaded[k], (j + 1) * 16)
                    row_stats(j, k)

            def sample(s, last):
                done = [0]

                def link(ins):
                    done[0] += 1
                    ins.then_inc(chain, 1)
                    dve.wait_ge(chain, s * CHAIN + done[0])

                for layer in range(LAYERS):
                    n_layer = s * LAYERS + layer + 1
                    dve.wait_ge(duo_stats, n_layer * DUOS)
                    settle(dve)
                    for h in range(HV):
                        last_agg = nc.vector.bn_aggr(agg[:, h, :], stats[:, h].rearrange("p g s -> p (g s)"))
                    last_agg.then_inc(agg_ready, 1)
                    dve.wait_ge(mean_ready, n_layer)
                    if layer == DENSE:
                        nc.vector.tensor_scalar(neg_mean[:], ps_mean, -1.0, None, ALU.mult).then_inc(affine_ready, 1)
                    else:
                        n_split = s * len(DEPTHWISE) + DEPTHWISE.index(layer) + 1
                        w_at = DEPTHWISE.index(layer)
                        link(nc.vector.tensor_tensor(dev[:], agg[:, :, 0], ps_mean, ALU.subtract))
                        link(nc.vector.tensor_tensor(spread[:], dev[:], dev[:], ALU.mult))
                        nc.vector.tensor_tensor(spread[:], spread[:], agg[:, :, 1], ALU.add).then_inc(spread_ready, 1)
                        dve.wait_ge(group_var_ready, n_split)
                        nc.vector.tensor_scalar(var[:], ps_var, GN_EPS, None, ALU.add).then_inc(var_ready, 1)
                        dve.wait_ge(std_ready, n_split)
                        link(nc.vector.reciprocal(rstd[:], std[:]))
                        link(nc.vector.tensor_tensor(newton[:], rstd[:], rstd[:], ALU.mult))
                        link(nc.vector.tensor_tensor(newton[:], newton[:], var[:], ALU.mult))
                        link(nc.vector.tensor_scalar(newton[:], newton[:], -0.5, 1.5, ALU.mult, ALU.add))
                        link(nc.vector.tensor_tensor(rstd[:], rstd[:], newton[:], ALU.mult))
                        nc.vector.tensor_tensor(pooled[:], dev[:], rstd[:], ALU.mult).then_inc(pooled_ready, 1)
                        link(nc.vector.tensor_scalar(x_mul[:], rstd[:], X_SCALE, None, ALU.mult))
                        nc.vector.scalar_tensor_tensor(x_add[:], ps_mean, -1.0, x_mul[:], ALU.mult, ALU.mult)\
                            .then_inc(affine_ready, 1)
                        dve.wait_ge(hidden_sum_ready, n_split)
                        nc.vector.tensor_scalar(hidden[:], ps_hidden.to_broadcast([HID, P]),
                                                b1_sb[:, w_at:w_at + 1], 0.0, ALU.add, ALU.max).then_inc(hidden_ready, 1)
                        dve.wait_ge(taps_ready, n_split)
                        for h in range(HV):
                            pick = nc.vector.tensor_tensor(
                                picked[:, h], ps_taps.rearrange("p (v c t) -> p v c t", v=HV, t=TAPS)[:, h],
                                same_ch.unsqueeze(2).to_broadcast([P, CH, TAPS]), ALU.mult)
                        link(pick)
                        link(nc.vector.tensor_reduce(taps[:], picked.rearrange("p v c t -> p v t c"), AX.X, ALU.add))
                        link(nc.vector.tensor_tensor(taps[:], taps[:], b2_sb[:, w_at], ALU.add))
                        link(nc.vector.tensor_reduce(tap_max[:], taps[:], AX.X, ALU.max, apply_absolute_value=True))
                        link(nc.vector.tensor_scalar(tap_max[:], tap_max[:], 1e-30, None, ALU.max))
                        nc.vector.tensor_scalar(out_mul[:], tap_max[:], 1.0 / (W_SCALE * X_SCALE), None, ALU.mult)
                        link(nc.vector.reciprocal(tap_inv[:], tap_max[:]))
                        for h in range(HV):
                            scaled = nc.vector.tensor_scalar(taps[:, h], taps[:, h], tap_inv[:, h:h + 1], W_SCALE,
                                                             ALU.mult, ALU.mult)
                        link(scaled)
                        link(nc.vector.tensor_copy(parts[:, :, 0], taps[:]))
                        link(nc.vector.tensor_tensor(parts[:, :, 1], taps[:], parts[:, :, 0], ALU.subtract))
                        shape = [P, 2, 3 * S * R, TAPS]
                        for h in range(HV):
                            mask = nc.vector.tensor_tensor(
                                masked[h], parts[:, h].unsqueeze(2).to_broadcast(shape),
                                use.rearrange("p k s (r t) -> p (k s r) t", t=TAPS).unsqueeze(1).to_broadcast(shape),
                                ALU.mult)
                        link(mask)
                        for h in range(HV):
                            place = nc.vector.tensor_reduce(by_place[:, h], masked[h], AX.X, ALU.add)
                        link(place)
                        for h in range(HV):
                            shape = [P, 2 * 3 * S, CH, R]
                            nc.vector.tensor_tensor(
                                w_split[:, h].rearrange("p a k (s c r) -> p (a k s) c r", s=S, r=R),
                                by_place[:, h].rearrange("p a (n r) -> p (a n) r", r=R).unsqueeze(2).to_broadcast(shape),
                                same_ch.unsqueeze(1).unsqueeze(3).to_broadcast(shape), ALU.mult)\
                                .then_inc(weights_ready, 1)

                    final = layer == LAYERS - 1
                    for step in steps(dve, EVAC_LAG if not final or last else STAT_LAG):
                        split = step.lagged(0) if layer != DENSE else None
                        if split:
                            j, k = split
                            for h in range(HV):
                                dve.wait_ge(high_ready[h], duo_count(s, layer, j, k) + 1)
                                spot = ring[:, :, h, k * DG:(k + 1) * DG, 1:WS + 1]
                                nc.vector.tensor_tensor(spot[:, 1], xn[:, h].rearrange("p (g w) -> p g w", g=DG),
                                                        spot[:, 0], ALU.subtract).then_inc(low_ready[h], 1)
                        add = step.lagged(EVAC_LAG)
                        if add:
                            j, k = add
                            uses = acc_uses(s, layer, j, k)
                            for h in range(HV):
                                dve.wait_ge(acc_full[k][h], slot_uses(s, layer, j) + 1)
                                dst = y[:, h, bass.ds(j * RG + k * DG, DG), :]\
                                    .rearrange("p (b g) w -> p b (g w)", g=BG)
                                src = acc[:, k % 2, h, :, 0:NB]
                                if layer == DENSE:
                                    ins = nc.vector.tensor_tensor(dst, src, dst, ALU.add)
                                else:
                                    ins = nc.vector.scalar_tensor_tensor(dst, src, out_mul[:, h:h + 1], dst,
                                                                         ALU.mult, ALU.add)
                                ins.then_inc(acc_free[k % 2][h], 1)
                            if not final:
                                for h in range(HV):
                                    dve.wait_ge(acc_free[k % 2][h], uses + 1)
                                row_stats(j, k)
                        arrived = step.lagged(STAT_LAG) if final and not last else None
                        if arrived:
                            j, k = arrived
                            dve.wait_ge(loaded[k], (s * TURNS + j + TURNS + 1) * 16)
                            row_stats(j, k)
                assert done[0] == CHAIN, done

            for_samples(dve, sample)

        @block.tensor
        def _(pe):
            pe.wait_ge(params_in, 16 * PARAM_DMAS)
            pe.wait_ge(setup_chain, 1)
            pe.wait_ge(dense_ready, 1)

            def small(out_, lhsT, rhs, start=True, stop=True):
                return nc.tensor.matmul(out_, lhsT, rhs, start=start, stop=stop)

            def sample(s, last):
                for layer in range(LAYERS):
                    n_layer = s * LAYERS + layer + 1
                    pe.wait_ge(agg_ready, n_layer)
                    small(ps_mean, pair_avg, agg[:, :, 0]).then_inc(mean_ready, 1)
                    if layer != DENSE:
                        w_at = DEPTHWISE.index(layer)
                        n_split = s * len(DEPTHWISE) + w_at + 1
                        pe.wait_ge(spread_ready, n_split)
                        small(ps_var, pair_avg, spread[:]).then_inc(group_var_ready, 1)
                        pe.wait_ge(pooled_ready, n_split)
                        for h in range(HV):
                            hid = small(ps_hidden, w1_sb[:, w_at, h, :], pooled[:, h:h + 1], h == 0, h == HV - 1)
                        hid.then_inc(hidden_sum_ready, 1)
                        pe.wait_ge(hidden_ready, n_split)
                        small(ps_taps, hidden[:], w2_sb[:, w_at, :]).then_inc(taps_ready, 1)
                        pe.wait_ge(weights_ready, n_split * HV)
                        settle(pe)
                    else:
                        pe.wait_ge(affine_ready, n_layer)
                        settle(pe)
                    with pe.Fori(0, TURNS) as j:
                        for k in range(SLOTS):
                            uses = acc_uses(s, layer, j, k)

                            def full(h, w, tile, first=False, last=False):
                                for bank in range(BANKS):
                                    src = tile[:, bank * BG:(bank + 1) * BG, 1:1 + WS]
                                    mm = nc.tensor.matmul(acc[:, k % 2, h, bank, 0:NB], w, src, start=first, stop=last)
                                return mm

                            def sides(h, w, tile):
                                for turn in range(BANKS):
                                    for left in (True, False):
                                        bank = turn if left else 1 - turn
                                        k0, m0, off = (64, 0, 0) if left else (0, 64, 2)
                                        src = tile[k0:k0 + 64, bank * BG:(bank + 1) * BG, off:off + WS]
                                        nc.tensor.matmul(acc[m0:m0 + 64, k % 2, h, bank, 0:NB],
                                                         w[k0:k0 + 64, m0:m0 + 64], src, start=False, stop=False)

                            now = slice(k * DG, (k + 1) * DG)
                            if layer == DENSE:
                                terms = [[(w_signs[:, v, h], ring[:, 0, v, now], halo[:, k % HALO_SLOTS, 0, v])
                                          for v in range(HV)] for h in range(HV)]
                                for h in range(HV):
                                    pe.wait_ge(high_ready[h], duo_count(s, layer, j, k) + 1)
                            else:
                                terms = [[(w_split[:, h, a_w], ring[:, a_x, h, now], halo[:, k % HALO_SLOTS, a_x, h])
                                          for a_w, a_x in ((0, 0), (0, 1), (1, 0))] for h in range(HV)]
                            for h in range(HV):
                                if layer != DENSE:
                                    pe.wait_ge(low_ready[h], split_count(s, layer, j, k) + 1)
                                pe.wait_ge(acc_free[k % 2][h], uses)
                                for n, (w, tile, _) in enumerate(terms[h]):
                                    full(h, w[:, CENTER], tile, first=(n == 0))
                            for h in range(HV):
                                for w, tile, _ in terms[h]:
                                    sides(h, w[:, SIDES], tile)
                            pe.wait_ge(halo_copied[k % HALO_SLOTS], halo_value(s, layer, j, k))
                            for h in range(HV):
                                for n, (w, _, edge) in enumerate(terms[h]):
                                    mm = full(h, w[:, EDGES], edge, last=(n == len(terms[h]) - 1))
                                mm.then_inc(acc_full[k][h], 1)
            for_samples(pe, sample)


PARAM_DMAS = 1 + 3 * (2 * S * R + 2)
CHAIN = 57


def kernel(**inputs):
    import concourse.bacc as bacc
    from concourse.bass_utils import run_bass_kernel_spmd

    def lay(a):
        return np.ascontiguousarray(a)

    xs = np.asarray(inputs["x"]).reshape(B, HV, CH, G, R, WS, S).transpose(0, 6, 2, 4, 1, 3, 5)
    arrays = {"x": lay(xs).reshape(B, P, HV, G, WS)}
    for n, name in enumerate(("L0", "L2", "L3")):
        for part in ("w1", "b1", "w2", "b2"):
            arrays[f"{part}_{n}"] = lay(inputs[f"{name}_conv_{part}"])
    arrays["w_dense"] = lay(np.asarray(inputs["L1_conv_W"]).reshape(C, C, TAPS).transpose(1, 0, 2)).reshape(C, C * TAPS)
    arrays["consts"] = shape_constants()

    nc = bacc.Bacc("TRN2", target_bir_lowering=False, num_devices=1)
    aps = {name: nc.dram_tensor(name, a.shape, mybir.dt.from_np(a.dtype), kind="ExternalInput").ap()
           for name, a in arrays.items()}
    out = nc.dram_tensor("out", (B, P, HV, G, WS), F32, kind="ExternalOutput").ap()
    conv_preact_kernel(nc, aps["x"], *([aps[f"{part}_{n}"] for n in range(3)] for part in ("w1", "b1", "w2", "b2")),
                       aps["w_dense"], aps["consts"], out)
    r = run_bass_kernel_spmd(nc, [arrays], core_ids=[0])
    got = r.results[0]["out"].reshape(B, S, CH, R, HV, G, WS).transpose(0, 4, 2, 5, 3, 6, 1)
    return lay(got).reshape(B, C, H, W)
```

```python
from contextlib import ExitStack

import numpy as np

import concourse.bass as bass
from concourse import mybir
from concourse.alu_op_type import AluOpType as ALU

ACT = mybir.ActivationFunctionType
AX = mybir.AxisListType
F32 = mybir.dt.float32
F16 = mybir.dt.float16

B, C, H, W = 8, 32, 384, 384
HID = 128
TAPS = 9
S = 2
R = 4
CH = 16
P = S * CH * R
HV = C // CH
G = H // R
WS = W // S
DG = 4
BG = 2
BANKS = DG // BG
NB = BG * WS
DUOS = G // DG
SLOTS = 4
HALO_SLOTS = 2
TURNS = DUOS // SLOTS
RG = SLOTS * DG
WP = WS + 2
LAYERS = 4
DENSE = 1
DEPTHWISE = [0, 2, 3]
GN_EPS = 1e-5
X_SCALE = 64.0
W_SCALE = 1024.0
STORE_LAG = 4
LOAD_LAG = 5
AHEAD = TURNS
AHEAD_LAYER = 2
CHUNKS = AHEAD * BANKS * HV
AHEAD_LAG = 4
AHEAD_STAT_LAG = 1
STAT_LAG = 4
EDGE_COPIES = 6
WRAP_COPIES = 3


IDLE_COLUMNS = 128
IDLE_PRODUCTS_STATS = 35
IDLE_PRODUCTS_POOLED = 30
IDLE_PRODUCTS_WEIGHTS = 55
IDLE_PRODUCTS_SIGNS = 35

CENTER, SIDES, EDGES = range(3)


def shape_constants():
    p = np.arange(P)
    parity, ch, row = p // (CH * R), p // R % CH, p % R
    pair = ((ch[:, None] // 2) == (ch[None, :] // 2)).astype(np.float32) / (2 * R * S)
    same = (ch[:, None] == np.arange(CH)[None, :]).astype(np.float32)
    use = np.zeros((P, 3, S, R, 3, 3), np.float32)
    for q in p:
        for s_out in range(S):
            for r_out in range(R):
                def enter(kind, y, x):
                    dy, dx = y - r_out, x - s_out
                    if abs(dy) <= 1 and abs(dx) <= 1:
                        use[q, kind, s_out, r_out, dy + 1, dx + 1] = 1.0
                enter(CENTER, row[q], parity[q])
                if s_out != parity[q]:
                    enter(SIDES, row[q], -1 if parity[q] else S)
                y = -1 if row[q] % 2 == 0 else R
                if row[q] < 2:
                    enter(EDGES, y, parity[q])
                elif s_out != parity[q]:
                    enter(EDGES, y, -1 if parity[q] else S)
    return np.concatenate([pair, same, use.reshape(P, -1)], axis=1).astype(np.float32)


C_SAME = P
C_USE = C_SAME + CH
C_ALL = C_USE + 3 * S * R * TAPS


def halo_value(s, layer, j, k):
    per_turn = EDGE_COPIES * SLOTS // HALO_SLOTS
    upto = EDGE_COPIES * (k // HALO_SLOTS + 1)
    return (s * (LAYERS * TURNS * per_turn) + j * per_turn + (layer * TURNS * per_turn + upto + per_turn)) * 16


def wrap_value(s, layer, j):
    return (s * (LAYERS * TURNS) + j + (layer * TURNS + 1)) * (WRAP_COPIES * 16)


class Step:

    def __init__(self, j, k, i):
        self.j, self.k, self.i = j, k, i

    def lagged(self, lag):
        if self.i is not None and not 0 <= self.i - lag < DUOS:
            return None
        return self.j + (self.k - lag) // SLOTS, (self.k - lag) % SLOTS


def steps(eng, lag, peeled_end=0, drain=True):
    peeled = -(-lag // SLOTS)
    for i in range(peeled * SLOTS):
        yield Step(i // SLOTS, i % SLOTS, i)
    with eng.Fori(peeled, TURNS - peeled_end) as j:
        for k in range(SLOTS):
            yield Step(j, k, None)
    for i in range((TURNS - peeled_end) * SLOTS, DUOS + (lag if drain else 0)):
        yield Step(i // SLOTS, i % SLOTS, i)


def for_samples(eng, body):
    with eng.Fori(0, B - 1) as s:
        body(s, False)
    body(B - 1, True)


def conv_preact_kernel(nc, x, w1, b1, w2, b2, w_dense, consts, out):
    ctx = ExitStack()
    with ctx:
        def sb(name, shape, dt):
            return ctx.enter_context(nc.sbuf_tensor(name, shape, dt))

        def sem(name):
            return ctx.enter_context(nc.semaphore(name))

        y = sb("y", [P, HV, G, WS], F32)
        ring = sb("ring", [P, 2, HV, RG, WP], F16)
        halo = sb("halo", [P, HALO_SLOTS, 2, HV, DG, WP], F16)
        zero_row = sb("zero_row", [S * CH, 2, HV, WP], F16)
        xn = sb("xn", [P, HV, DG * WS], F32)
        w_split = sb("w_split", [P, HV, 2, 3, P], F16)
        w_signs = sb("w_signs", [P, HV, HV, 3, P], F16)
        cst = sb("cst", [P, C_ALL], F32)
        w1_sb = sb("w1_sb", [P, 3, HV, HID], F32)
        w2_sb = sb("w2_sb", [HID, 3, C * TAPS], F32)
        b1_sb = sb("b1_sb", [HID, 3], F32)
        b2_sb = sb("b2_sb", [P, 3, HV, TAPS], F32)
        stats = sb("stats", [P, HV, G // BG, 6], F32)
        ahead = sb("ahead", [P, NB], F32)
        ahead_stats = sb("ahead_stats", [P, HV, AHEAD * BANKS, 6], F32)
        agg = sb("agg", [P, HV, 2], F32)
        dev = sb("dev", [P, HV], F32)
        spread = sb("spread", [P, HV], F32)
        var = sb("var", [P, HV], F32)
        std = sb("std", [P, HV], F32)
        rstd = sb("rstd", [P, HV], F32)
        newton = sb("newton", [P, HV], F32)
        x_mul = sb("x_mul", [P, HV], F32)
        x_add = sb("x_add", [P, HV], F32)
        neg_mean = sb("neg_mean", [P, HV], F32)
        pooled = sb("pooled", [P, HV], F32)
        hidden = sb("hidden", [HID, P], F32)
        taps = sb("taps", [P, HV, TAPS], F32)
        tap_max = sb("tap_max", [P, HV], F32)
        tap_inv = sb("tap_inv", [P, HV], F32)
        out_mul = sb("out_mul", [P, HV], F32)
        parts = sb("parts", [P, HV, 2, TAPS], F16)
        by_place = sb("by_place", [P, HV, 2, 3 * S * R], F32)
        acc = ctx.enter_context(nc.psum_tensor("acc", [P, 2, HV, BANKS, 512], F32))

        dense_raw = [xn[:, 0, v * C * TAPS:(v + 1) * C * TAPS] for v in range(HV)]
        stage = xn[:, 1, 0:C * TAPS]
        ps_mean = acc[:, 0, 0, 0, 504:504 + HV]
        ps_var = acc[:, 0, 0, 1, 504:504 + HV]
        ps_hidden = acc[:, 0, 1, 0, 504:505]
        ps_taps = acc[:, 0, 1, 1, 0:C * TAPS]
        picked = acc[:, 0, 0, 0, 0:C * TAPS].rearrange("p (v c t) -> p v c t", v=HV, t=TAPS)
        masked = [acc[:, 0, h, 1 - h, 0:2 * 3 * S * R * TAPS].rearrange("p (a n t) -> p a n t", a=2, t=TAPS)
                  for h in range(HV)]

        pair_avg = cst[:, 0:P]
        same_ch = cst[:, C_SAME:C_USE]
        use = cst[:, C_USE:C_ALL].rearrange("p (k s n) -> p k s n", k=3, s=S)

        def replicas():
            for s in range(S):
                for r in range(R):
                    first = s * CH * R + r
                    yield slice(first, first + (CH - 1) * R + 1, R)

        params_in = sem("params_in")
        dense_in = [sem(f"dense_in{v}") for v in range(HV)]
        cleared = sem("cleared")
        setup_chain = sem("setup_chain")
        dense_ready = sem("dense_ready")
        duo_stats = sem("duo_stats")
        chain = sem("chain")
        loaded = [sem(f"loaded{k}") for k in range(SLOTS)]
        stored = [sem(f"stored{k}") for k in range(SLOTS)]
        ahead_in = sem("ahead_in")
        ahead_used = sem("ahead_used")
        agg_ready = sem("agg_ready")
        mean_ready = sem("mean_ready")
        spread_ready = sem("spread_ready")
        group_var_ready = sem("group_var_ready")
        var_ready = sem("var_ready")
        std_ready = sem("std_ready")
        affine_ready = sem("affine_ready")
        pooled_ready = sem("pooled_ready")
        hidden_sum_ready = sem("hidden_sum_ready")
        hidden_ready = sem("hidden_ready")
        taps_ready = sem("taps_ready")
        weights_ready = sem("weights_ready")
        xn_ready = sem("xn_ready")
        high_ready = [sem(f"high_ready{h}") for h in range(HV)]
        low_ready = [sem(f"low_ready{h}") for h in range(HV)]
        halo_copied = [sem(f"halo_copied{k}") for k in range(HALO_SLOTS)]
        acc_full = [[sem(f"acc_full{k}{h}") for h in range(HV)] for k in range(SLOTS)]
        halo_wrapped = {0: sem("halo_wrapped_above"), SLOTS - 1: sem("halo_wrapped_below")}
        wrap_below_seen = sem("wrap_below_seen")
        ring_released = [acc_full[k][HV - 1] for k in range(SLOTS)]
        acc_free = [[sem(f"acc_free{q}{h}") for h in range(HV)] for q in range(2)]

        wait_carrier = sem("wait_carrier")

        def settle(eng):
            eng.sem_inc(wait_carrier, 1)

        credited = [*(x for pair in acc_full + acc_free for x in pair), *low_ready, wrap_below_seen, ahead_used]

        def duo_count(s, layer, j, k):
            return s * (LAYERS * DUOS) + j * SLOTS + (layer * DUOS + k)

        def split_count(s, layer, j, k):
            return s * (len(DEPTHWISE) * DUOS) + j * SLOTS + (DEPTHWISE.index(layer) * DUOS + k + 1)

        def slot_uses(s, layer, j):
            return s * (LAYERS * TURNS) + j + (layer * TURNS + 1)

        def seen_count(s, layer, j):
            return s * (LAYERS * (TURNS - 1)) + j + (layer * (TURNS - 1) + 1)

        def acc_uses(s, layer, j, k):
            return s * (LAYERS * DUOS // 2) + j * (SLOTS // 2) + (layer * DUOS // 2 + k // 2 + 1)

        def chunks_before(s, j, k):
            return s * CHUNKS + j * SLOTS + k

        def duo_rows(j, k):
            return y[:, :, bass.ds(j * RG + k * DG, DG), :]

        def wait_halo_free(eng, s, layer, j, k):
            before = (k - HALO_SLOTS) % SLOTS
            eng.wait_ge(ring_released[before], slot_uses(s, layer, j) + (0 if k < HALO_SLOTS else 1))
            settle(eng)

        def copy_edge(eng, layer, k, below, g, ng, src):
            done = halo_wrapped[k] if (below, g, ng) in ((0, 0, 1), (1, DG - 1, 1)) else halo_copied[k % HALO_SLOTS]
            tile = halo[:, k % HALO_SLOTS].rearrange("p a v g w -> p (a v) (g w)")
            held = ring[:].rearrange("p a v g w -> p (a v) (g w)")
            zeros = zero_row[:].rearrange("p a v w -> p (a v) w")
            nv = HV if layer == DENSE else 2 * HV
            row = 0 if below else R - 1
            for part0, n, place, shift in ((0, S * CH, below, 0), (0, CH, 2 + below, -1), (CH, CH, 2 + below, 1)):
                size = ng * WP - abs(shift)
                at = slice(part0 * R + place, (part0 + n - 1) * R + place + 1, R)
                from_at = slice(part0 * R + row, (part0 + n - 1) * R + row + 1, R)
                d0, s0 = max(shift, 0), max(-shift, 0)
                dst = tile[at, 0:nv, g * WP + d0:g * WP + d0 + size]
                if src is None:
                    from_ = zeros[0:n, 0:nv, s0:s0 + size]
                else:
                    from_ = held[from_at, 0:nv, src * WP + s0:src * WP + s0 + size]
                eng.dma_start(dst, from_).then_inc(done, 16)

        block = ctx.enter_context(nc.Block())

        @block.sync
        def _(sp):
            def load(s, j, k):
                sp.dma_start(duo_rows(j, k), x[s, :, :, bass.ds(j * RG + k * DG, DG), :]).then_inc(loaded[k], 16)

            for i in range(SLOTS):
                load(0, 0, i)
            with sp.Fori(1, TURNS) as j:
                for k in range(SLOTS):
                    sp.wait_ge(loaded[k], j * 16)
                    load(0, j, k)
            def copy_halo(s, layer, j, k):
                wait_halo_free(sp, s, layer, j, k)
                for below in (0, 1):
                    g0, ng = (1, DG - 1) if not below and k == 0 else (0, DG - (below and k == SLOTS - 1))
                    copy_edge(sp, layer, k, below, g0, ng, k * DG + g0 + (1 if below else -1))

            def sample(s, last):
                for layer in range(LAYERS):
                    final = layer == LAYERS - 1
                    looks_ahead = layer == AHEAD_LAYER and not last
                    lag = AHEAD_LAG if looks_ahead else 1 if not final else STORE_LAG if last else LOAD_LAG
                    for step in steps(sp, lag):
                        made = step.lagged(0)
                        if made:
                            if layer == DENSE:
                                for h in range(HV):
                                    sp.wait_ge(high_ready[h], duo_count(s, layer, *made) + 1)
                                    settle(sp)
                            else:
                                for h in range(HV):
                                    sp.wait_ge(low_ready[h], split_count(s, layer, *made) + 1)
                                    settle(sp)
                        target = step.lagged(1)
                        if target:
                            copy_halo(s, layer, *target)
                        chunk = step.lagged(AHEAD_LAG) if looks_ahead else None
                        if chunk:
                            j, k = chunk
                            sp.wait_ge(ahead_used, chunks_before(s, j, k) + 1)
                            settle(sp)
                            first = (DUOS - AHEAD) * DG + j * DG + (k // HV) * BG
                            sp.dma_start(ahead[:], x[s + 1, :, k % HV, bass.ds(first, BG), :]
                                         .rearrange("p g w -> p (g w)")).then_inc(ahead_in, 16)
                        done = step.lagged(STORE_LAG) if final else None
                        if done:
                            j, k = done
                            for h in range(HV):
                                sp.wait_ge(acc_free[k % 2][h], acc_uses(s, layer, j, k) + 1)
                                settle(sp)
                            sp.dma_start(out[s, :, :, bass.ds(j * RG + k * DG, DG), :], duo_rows(j, k))\
                                .then_inc(stored[k], 16)
                        gone = step.lagged(LOAD_LAG) if final and not last else None
                        if gone:
                            j, k = gone
                            sp.wait_ge(stored[k], (s * TURNS + j + 1) * 16)
                            settle(sp)
                            sp.wait_ge(loaded[k], (s * TURNS + j + TURNS) * 16)
                            settle(sp)
                            load(s + 1, j, k)

            sp.wait_ge(cleared, 2)
            for_samples(sp, sample)
            for k in range(SLOTS):
                sp.wait_ge(stored[k], B * TURNS * 16)

        @block.gpsimd
        def _(pool):
            for start in credited:
                pool.sem_inc(start, 1)
            for start in halo_copied:
                pool.sem_inc(start, 16 * EDGE_COPIES * SLOTS // HALO_SLOTS)
            pool.memset(ring[:].rearrange("p a v g w -> p (a v g w)").bitcast(F32), 0.0).then_inc(cleared, 1)
            pool.memset(zero_row[:].rearrange("p a v w -> p (a v w)").bitcast(F32), 0.0).then_inc(cleared, 1)
            pool.wait_ge(cleared, 2)

            def sample(s, last):
                for layer in range(LAYERS):
                    wait_halo_free(pool, s, layer, 0, 0)
                    copy_edge(pool, layer, 0, 0, 0, 1, None)
                    for step in steps(pool, 1):
                        made = step.lagged(0)
                        if made and layer != DENSE:
                            j, k = made
                            for h in range(HV):
                                pool.wait_ge(high_ready[h], duo_count(s, layer, j, k) + 1)
                                spot = ring[:, :, h, k * DG:(k + 1) * DG, 1:WS + 1]
                                nc.gpsimd.tensor_tensor(spot[:, 1], xn[:, h].rearrange("p (g w) -> p g w", g=DG),
                                                        spot[:, 0], ALU.subtract).then_inc(low_ready[h], 1)
                        if made and made[1] == 1 and not (isinstance(made[0], int) and made[0] == 0):
                            pool.wait_ge(halo_wrapped[SLOTS - 1], wrap_value(s, layer, made[0] - 1))
                            settle(pool)
                            pool.sem_inc(wrap_below_seen, 1)
                        target = step.lagged(1)
                        if target and target[1] in halo_wrapped and step.i != 1:
                            j, k = target
                            wait_halo_free(pool, s, layer, j, k)
                            if made:
                                for h in range(HV):
                                    if layer == DENSE:
                                        pool.wait_ge(high_ready[h], duo_count(s, layer, *made) + 1)
                                    else:
                                        pool.wait_ge(low_ready[h], split_count(s, layer, *made) + 1)
                                    settle(pool)
                            if k == 0:
                                copy_edge(pool, layer, k, 0, 0, 1, RG - 1)
                            else:
                                copy_edge(pool, layer, k, 1, DG - 1, 1,
                                          None if isinstance(j, int) and j == TURNS - 1 else 0)

            for_samples(pool, sample)

        @block.scalar
        def _(act):
            act.dma_start(cst[:], consts).then_inc(params_in, 16)
            for n in range(3):
                for at in replicas():
                    act.dma_start(w1_sb[at, n], w1[n].rearrange("(v c) m -> c v m", v=HV)).then_inc(params_in, 16)
                    act.dma_start(b2_sb[at, n], b2[n].rearrange("(v c t) -> c v t", v=HV, t=TAPS))\
                        .then_inc(params_in, 16)
                act.dma_start(w2_sb[:, n, :], w2[n]).then_inc(params_in, 16)
                act.dma_start(b1_sb[:, n:n + 1], b1[n].rearrange("(m a) -> m a", a=1)).then_inc(params_in, 16)
            for v in range(HV):
                for at in replicas():
                    act.dma_start(dense_raw[v][at, :], w_dense[v * CH:(v + 1) * CH, :]).then_inc(dense_in[v], 16)
            act.wait_ge(cleared, 2)
            act.wait_ge(dense_ready, 1)

            def sample(s, last):
                for layer in range(LAYERS):
                    if layer != DENSE:
                        act.wait_ge(var_ready, s * len(DEPTHWISE) + DEPTHWISE.index(layer) + 1)
                        nc.scalar.activation(std[:], var[:], ACT.Sqrt).then_inc(std_ready, 1)
                    act.wait_ge(affine_ready, s * LAYERS + layer + 1)
                    def turn(j):
                        for k in range(SLOTS):
                            act.wait_ge(ring_released[k], slot_uses(s, layer, j))
                            k_next = (k + 1) % SLOTS
                            j_next = j if k == SLOTS - 1 else j - 1
                            if k_next > 0 or not isinstance(j, int):
                                act.wait_ge(halo_copied[k_next % HALO_SLOTS], halo_value(s, layer, j_next, k_next))
                                if k_next == 0:
                                    act.wait_ge(halo_wrapped[k_next], wrap_value(s, layer, j))
                            if k_next == SLOTS - 1:
                                act.wait_ge(wrap_below_seen, seen_count(s, layer, j))
                            for h in range(HV):
                                if layer == 0 and h == 0:
                                    act.wait_ge(loaded[k], (s * TURNS + j + 1) * 16)
                                src = y[:, h, bass.ds(j * RG + k * DG, DG), :]
                                dst = ring[:, 0, h, k * DG:(k + 1) * DG, 1:WS + 1]
                                if layer == DENSE:
                                    nc.scalar.activation(dst, src, ACT.Sign, bias=neg_mean[:, h:h + 1])\
                                        .then_inc(high_ready[h], 1)
                                    continue
                                n = split_count(s, layer, j, k)
                                held = xn[:, h].rearrange("p (g w) -> p g w", g=DG)
                                act.wait_ge(low_ready[h], n)
                                nc.scalar.activation(held, src, ACT.Identity, bias=x_add[:, h:h + 1],
                                                     scale=x_mul[:, h:h + 1]).then_inc(xn_ready, 1)
                                act.wait_ge(xn_ready, (n - 1) * HV + h + 1)
                                nc.scalar.copy(dst, held).then_inc(high_ready[h], 1)

                    turn(0)
                    with act.Fori(1, TURNS) as j:
                        turn(j)

            for_samples(act, sample)

        @block.vector
        def _(dve):
            count = [0]

            def bank_stats(h, j, k):
                for bank in range(BANKS):
                    ins = nc.vector.bn_stats(
                        stats[:, h, bass.ds(j * (SLOTS * BANKS) + (k * BANKS + bank), 1), :]
                        .rearrange("p a b -> p (a b)"),
                        y[:, h, bass.ds(j * RG + (k * DG + bank * BG), BG), :].rearrange("p a b -> p (a b)"))
                return ins

            def row_stats(j, k):
                for h in range(HV):
                    ins = bank_stats(h, j, k)
                ins.then_inc(duo_stats, 1)

            def chunk_stats(s, j, k):
                dve.wait_ge(ahead_in, (chunks_before(s, j, k) + 1) * 16)
                nc.vector.bn_stats(ahead_stats[:, k % HV, bass.ds(j * BANKS + k // HV, 1), :].rearrange("p a b -> p (a b)"),
                                   ahead[:]).then_inc(ahead_used, 1)

            with dve.Fori(0, TURNS) as j:
                for k in range(SLOTS):
                    dve.wait_ge(loaded[k], (j + 1) * 16)
                    row_stats(j, k)

            def setup(ins):
                count[0] += 1
                ins.then_inc(setup_chain, 1)
                dve.wait_ge(setup_chain, count[0])

            dve.wait_ge(params_in, 16 * PARAM_DMAS)
            setup(nc.vector.tensor_scalar(w1_sb[:], w1_sb[:], 1.0 / (S * R), None, ALU.mult))

            signs = stage.rearrange("p (o t) -> p o t", t=TAPS)
            for v in range(HV):
                dve.wait_ge(dense_in[v], 16 * S * R)
                setup(nc.vector.tensor_scalar(stage, dense_raw[v], 0.0, None, ALU.is_lt))
                setup(nc.vector.scalar_tensor_tensor(stage, dense_raw[v], 0.0, stage, ALU.is_gt, ALU.subtract))
                for h in range(HV):
                    for kind in range(3):
                        for s_out in range(S):
                            for c0 in range(0, CH, CH // 2):
                                shape = [P, CH // 2, R, TAPS]
                                term = acc[:, 0, 0, (c0 > 0) * 1, 0:CH // 2 * R * TAPS]\
                                    .rearrange("p (c r t) -> p c r t", r=R, t=TAPS)
                                o = h * CH + c0
                                setup(nc.vector.tensor_tensor(
                                    term, signs[:, o:o + CH // 2, :].unsqueeze(2).to_broadcast(shape),
                                    use[:, kind, s_out, :].rearrange("p (r t) -> p r t", r=R).unsqueeze(1)
                                    .to_broadcast(shape), ALU.mult))
                                dst = w_signs[:, v, h, kind, :].rearrange("p (s c r) -> p s c r", s=S, r=R)
                                with nc.allow_low_precision(reason="one term of each sum is not zero"):
                                    nc.vector.tensor_reduce(dst[:, s_out, c0:c0 + CH // 2, :], term, AX.X, ALU.add)
            setup(nc.vector.memset(tap_max[:], 0.0))
            dve.sem_inc(dense_ready, 1)

            links = [0, 0]

            def link(ins, s=None):
                ins.then_inc(chain, 1)
                if s is None:
                    links[0] += 1
                    dve.wait_ge(chain, links[0])
                else:
                    links[1] += 1
                    dve.wait_ge(chain, s * CHAIN + (links[0] + links[1]))

            def aggregate(h):
                return nc.vector.bn_aggr(agg[:, h, :], stats[:, h].rearrange("p g s -> p (g s)"))

            def head(s, n_layer, n_split, w_at):
                dve.wait_ge(mean_ready, n_layer)
                link(nc.vector.tensor_tensor(dev[:], agg[:, :, 0], ps_mean, ALU.subtract), s)
                link(nc.vector.tensor_tensor(spread[:], dev[:], dev[:], ALU.mult), s)
                nc.vector.tensor_tensor(spread[:], spread[:], agg[:, :, 1], ALU.add).then_inc(spread_ready, 1)
                dve.wait_ge(group_var_ready, n_split)
                nc.vector.tensor_scalar(var[:], ps_var, GN_EPS, None, ALU.add).then_inc(var_ready, 1)
                dve.wait_ge(std_ready, n_split)
                link(nc.vector.reciprocal(rstd[:], std[:]), s)
                link(nc.vector.scalar_tensor_tensor(newton[:], rstd[:], -0.5, rstd[:], ALU.mult, ALU.mult), s)
                link(nc.vector.tensor_tensor(newton[:], newton[:], var[:], ALU.mult), s)
                link(nc.vector.scalar_tensor_tensor(rstd[:], newton[:], 1.5, rstd[:], ALU.add, ALU.mult), s)
                nc.vector.tensor_tensor(pooled[:], dev[:], rstd[:], ALU.mult).then_inc(pooled_ready, 1)
                link(nc.vector.tensor_scalar(x_mul[:], rstd[:], X_SCALE, None, ALU.mult), s)
                nc.vector.scalar_tensor_tensor(x_add[:], ps_mean, -1.0, x_mul[:], ALU.mult, ALU.mult)\
                    .then_inc(affine_ready, 1)
                dve.wait_ge(hidden_sum_ready, n_split)
                nc.vector.tensor_scalar(hidden[:], ps_hidden.to_broadcast([HID, P]),
                                        b1_sb[:, w_at:w_at + 1], 0.0, ALU.add, ALU.max).then_inc(hidden_ready, 1)

            dve.wait_ge(duo_stats, DUOS)
            for h in range(HV):
                last_agg = aggregate(h)
            last_agg.then_inc(agg_ready, 1)
            head(None, 1, 1, 0)

            def sample(s, last):
                links[1] = 0

                for layer in range(LAYERS):
                    n_layer = s * LAYERS + layer + 1
                    if layer == DENSE:
                        dve.wait_ge(mean_ready, n_layer)
                        nc.vector.tensor_scalar(neg_mean[:], ps_mean, -1.0, None, ALU.mult).then_inc(affine_ready, 1)
                    else:
                        n_split = s * len(DEPTHWISE) + DEPTHWISE.index(layer) + 1
                        w_at = DEPTHWISE.index(layer)
                        if layer > 0:
                            head(s, n_layer, n_split, w_at)
                        if layer == AHEAD_LAYER + 1 and not last:
                            chunk_stats(s, TURNS - 1, SLOTS - 2)
                        dve.wait_ge(taps_ready, n_split)
                        for h in range(HV):
                            pick = nc.vector.tensor_tensor(
                                picked[:, h], ps_taps.rearrange("p (v c t) -> p v c t", v=HV, t=TAPS)[:, h],
                                same_ch.unsqueeze(2).to_broadcast([P, CH, TAPS]), ALU.mult)
                        link(pick, s)
                        link(nc.vector.tensor_reduce(taps[:], picked.rearrange("p v c t -> p v t c"), AX.X, ALU.add), s)
                        link(nc.vector.tensor_tensor(taps[:], taps[:], b2_sb[:, w_at], ALU.add), s)
                        link(nc.vector.tensor_reduce(tap_max[:], taps[:], AX.X, ALU.max, apply_absolute_value=True), s)
                        link(nc.vector.tensor_scalar(tap_max[:], tap_max[:], 1.0 / W_SCALE, 1e-30, ALU.mult, ALU.max), s)
                        link(nc.vector.reciprocal(tap_inv[:], tap_max[:]), s)
                        for h in range(HV):
                            high = nc.vector.tensor_scalar(parts[:, h, 0], taps[:, h], tap_inv[:, h:h + 1], None,
                                                           ALU.mult)
                        link(high, s)
                        for h in range(HV):
                            low = nc.vector.scalar_tensor_tensor(parts[:, h, 1], taps[:, h], tap_inv[:, h:h + 1],
                                                                 parts[:, h, 0], ALU.mult, ALU.subtract)
                        link(low, s)
                        for h in range(HV):
                            shape = [P, 2, 3 * S * R, TAPS]
                            link(nc.vector.tensor_tensor(
                                masked[h], parts[:, h].unsqueeze(2).to_broadcast(shape),
                                use.rearrange("p k s (r t) -> p (k s r) t", t=TAPS).unsqueeze(1).to_broadcast(shape),
                                ALU.mult), s)
                            link(nc.vector.tensor_reduce(by_place[:, h], masked[h], AX.X, ALU.add), s)
                            shape = [P, 2 * 3 * S, CH, R]
                            nc.vector.tensor_tensor(
                                w_split[:, h].rearrange("p a k (s c r) -> p (a k s) c r", s=S, r=R),
                                by_place[:, h].rearrange("p a (n r) -> p (a n) r", r=R).unsqueeze(2).to_broadcast(shape),
                                same_ch.unsqueeze(1).unsqueeze(3).to_broadcast(shape), ALU.mult)\
                                .then_inc(weights_ready, 1)
                        link(nc.vector.tensor_scalar(out_mul[:], tap_max[:], 1.0 / X_SCALE, None, ALU.mult), s)
                        settle(dve)

                    final = layer == LAYERS - 1
                    looks_ahead = layer == AHEAD_LAYER and not last
                    if layer == AHEAD_LAYER + 1 and not last:
                        chunk_stats(s, TURNS - 1, SLOTS - 1)
                        dve.wait_ge(ahead_used, chunks_before(s, TURNS - 1, SLOTS - 1) + 2)
                        settle(dve)
                        nc.vector.tensor_copy(
                            stats[:, :, (DUOS - AHEAD) * BANKS:, :].rearrange("p v g s -> p v (g s)"),
                            ahead_stats[:].rearrange("p v g s -> p v (g s)")).then_inc(duo_stats, AHEAD)
                    loop = steps(dve, STAT_LAG, 1, False) if final and not last else \
                        steps(dve, 0) if final else \
                        steps(dve, AHEAD_STAT_LAG if looks_ahead else 0, 1, False)
                    for step in loop:
                        j, k = step.j, step.k
                        uses = acc_uses(s, layer, j, k)

                        def add(h):
                            dve.wait_ge(acc_full[k][h], slot_uses(s, layer, j) + 1)
                            dst = y[:, h, bass.ds(j * RG + k * DG, DG), :]\
                                .rearrange("p (b g) w -> p b (g w)", g=BG)
                            src = acc[:, k % 2, h, :, 0:NB]
                            if layer == DENSE:
                                ins = nc.vector.tensor_tensor(dst, src, dst, ALU.add)
                            else:
                                ins = nc.vector.scalar_tensor_tensor(dst, src, out_mul[:, h:h + 1], dst,
                                                                     ALU.mult, ALU.add)
                            ins.then_inc(acc_free[k % 2][h], 1)

                        if step.i == DUOS - 1 and not final:
                            for h in range(HV):
                                add(h)
                                dve.wait_ge(acc_free[k % 2][h], uses + 1)
                                ins = bank_stats(h, j, k)
                                if h == 0:
                                    link(ins, s)
                                    dve.wait_ge(duo_stats, n_layer * DUOS + (DUOS - 1))
                                else:
                                    ins.then_inc(duo_stats, 1)
                                    dve.wait_ge(duo_stats, n_layer * DUOS + DUOS)
                                settle(dve)
                                last_agg = aggregate(h)
                            last_agg.then_inc(agg_ready, 1)
                            continue
                        for h in range(HV):
                            add(h)
                        if not final:
                            for h in range(HV):
                                dve.wait_ge(acc_free[k % 2][h], uses + 1)
                            row_stats(j, k)
                        chunk = step.lagged(AHEAD_STAT_LAG) if looks_ahead else None
                        if chunk:
                            chunk_stats(s, *chunk)
                        if final and not last:
                            arrived = step.lagged(STAT_LAG)
                            if arrived and not (step.i and step.i - STAT_LAG >= DUOS - AHEAD):
                                dve.wait_ge(loaded[arrived[1]], (s * TURNS + arrived[0] + TURNS + 1) * 16)
                                row_stats(*arrived)
                            if step.i == DUOS - 3:
                                dve.wait_ge(duo_stats, n_layer * DUOS + DUOS)
                                settle(dve)
                                for h in range(HV):
                                    last_agg = aggregate(h)
                                last_agg.then_inc(agg_ready, 1)
                            if step.i == DUOS - 2:
                                head(s, n_layer + 1, n_split + 1, 0)
                assert last or links[1] == CHAIN, links

            for_samples(dve, sample)

        @block.tensor
        def _(pe):
            pe.wait_ge(params_in, 16 * PARAM_DMAS)
            pe.wait_ge(setup_chain, 1)
            pe.wait_ge(dense_ready, 1)

            def small(out_, lhsT, rhs, start=True, stop=True):
                return nc.tensor.matmul(out_, lhsT, rhs, start=start, stop=stop)

            def keep_clock(products, bank):
                for _ in range(products):
                    nc.tensor.matmul(bank[:, 0:IDLE_COLUMNS], w_signs[:, 0, 0, CENTER],
                                     w_signs[:, 0, 0, EDGES, 0:IDLE_COLUMNS], start=True, stop=True)

            def group_means(n_layer):
                pe.wait_ge(agg_ready, n_layer)
                small(ps_mean, pair_avg, agg[:, :, 0]).then_inc(mean_ready, 1)

            def group_variances(n_split):
                pe.wait_ge(spread_ready, n_split)
                small(ps_var, pair_avg, spread[:]).then_inc(group_var_ready, 1)

            def hidden_sums(n_split, w_at):
                pe.wait_ge(pooled_ready, n_split)
                for h in range(HV):
                    hid = small(ps_hidden, w1_sb[:, w_at, h, :], pooled[:, h:h + 1], h == 0, h == HV - 1)
                hid.then_inc(hidden_sum_ready, 1)

            group_means(1)
            group_variances(1)
            hidden_sums(1, 0)

            def sample(s, last):
                for layer in range(LAYERS):
                    n_layer = s * LAYERS + layer + 1
                    if layer > 0:
                        group_means(n_layer)
                    if layer != DENSE:
                        w_at = DEPTHWISE.index(layer)
                        n_split = s * len(DEPTHWISE) + w_at + 1
                        if layer > 0:
                            group_variances(n_split)
                            hidden_sums(n_split, w_at)
                        pe.wait_ge(hidden_ready, n_split)
                        small(ps_taps, hidden[:], w2_sb[:, w_at, :]).then_inc(taps_ready, 1)
                        pe.wait_ge(acc_free[1][0], acc_uses(s, layer, 0, 1))
                        keep_clock(IDLE_PRODUCTS_WEIGHTS, acc[:, 1, 0, 0])
                    else:
                        keep_clock(IDLE_PRODUCTS_SIGNS, acc[:, 0, 1, 1])
                        pe.wait_ge(affine_ready, n_layer)
                        settle(pe)

                    def terms(h, k):
                        now = slice(k * DG, (k + 1) * DG)
                        if layer == DENSE:
                            return [(w_signs[:, v, h], ring[:, 0, v, now], halo[:, k % HALO_SLOTS, 0, v])
                                    for v in range(HV)]
                        return [(w_split[:, h, a_w], ring[:, a_x, h, now], halo[:, k % HALO_SLOTS, a_x, h])
                                for a_w, a_x in ((0, 0), (0, 1), (1, 0))]

                    def full(h, k, w, tile, first=False, last=False):
                        for bank in range(BANKS):
                            src = tile[:, bank * BG:(bank + 1) * BG, 1:1 + WS]
                            mm = nc.tensor.matmul(acc[:, k % 2, h, bank, 0:NB], w, src, start=first, stop=last)
                        return mm

                    def sides(h, k, w, tile):
                        for turn in range(BANKS):
                            for left in (True, False):
                                bank = turn if left else 1 - turn
                                k0, m0, off = (64, 0, 0) if left else (0, 64, 2)
                                src = tile[k0:k0 + 64, bank * BG:(bank + 1) * BG, off:off + WS]
                                nc.tensor.matmul(acc[m0:m0 + 64, k % 2, h, bank, 0:NB],
                                                 w[k0:k0 + 64, m0:m0 + 64], src, start=False, stop=False)

                    def produced(h, j, k):
                        if layer == DENSE:
                            pe.wait_ge(high_ready[h], duo_count(s, layer, j, k) + 1)
                        else:
                            if isinstance(j, int) and j == 0 and k == 0:
                                pe.wait_ge(weights_ready, (n_split - 1) * HV + h + 1)
                            pe.wait_ge(low_ready[h], split_count(s, layer, j, k) + 1)

                    def centers(h, j, k):
                        pe.wait_ge(acc_free[k % 2][h], acc_uses(s, layer, j, k))
                        for n, (w, tile, _) in enumerate(terms(h, k)):
                            full(h, k, w[:, CENTER], tile, first=(n == 0))

                    def all_sides(h, k):
                        for w, tile, _ in terms(h, k):
                            sides(h, k, w[:, SIDES], tile)

                    def inside(j, k, small_between=None):
                        if layer == DENSE:
                            for h in range(HV):
                                produced(h, j, k)
                        for h in range(HV):
                            if layer != DENSE:
                                produced(h, j, k)
                            centers(h, j, k)
                            if isinstance(j, int) and j == 0 and k == 0:
                                all_sides(h, k)
                        if small_between:
                            small_between()
                        if not (isinstance(j, int) and j == 0 and k == 0):
                            for h in range(HV):
                                all_sides(h, k)

                    def halo_in(j, k):
                        pe.wait_ge(halo_copied[k % HALO_SLOTS], halo_value(s, layer, j, k))
                        if k in halo_wrapped:
                            pe.wait_ge(halo_wrapped[k], wrap_value(s, layer, j))

                    def half_edges(h, k):
                        of = terms(h, k)
                        for n, (w, _, tile) in enumerate(of):
                            mm = full(h, k, w[:, EDGES], tile, last=(n == len(of) - 1))
                        mm.then_inc(acc_full[k][h], 1)

                    def edges(j, k):
                        halo_in(j, k)
                        for h in range(HV):
                            half_edges(h, k)

                    inside(0, 0)
                    inside(0, 1)
                    edges(0, 0)
                    edges(0, 1)
                    for k in range(2, SLOTS):
                        inside(0, k)
                        edges(0, k)
                    with pe.Fori(1, TURNS - 1) as j:
                        for k in range(SLOTS):
                            inside(j, k)
                            edges(j, k)
                    j = TURNS - 1
                    for k in range(SLOTS - 1):
                        inside(j, k)
                        edges(j, k)
                    k = SLOTS - 1
                    if layer < LAYERS - 1:
                        for h in range(HV):
                            produced(h, j, k)
                        for h in range(HV):
                            centers(h, j, k)
                            all_sides(h, k)
                            if h == 0:
                                halo_in(j, k)
                            half_edges(h, k)
                        pe.wait_ge(acc_free[0][1], acc_uses(s, layer, j, k) + 1)
                        keep_clock(IDLE_PRODUCTS_STATS, acc[:, 0, 1, 1])
                    elif last:
                        inside(j, k)
                        edges(j, k)
                    else:
                        def means_between():
                            for h in range(HV):
                                pe.wait_ge(acc_free[0][h], acc_uses(s, layer, j, k) + 1)
                            settle(pe)
                            group_means(n_layer + 1)
                        inside(j, k, means_between)
                        group_variances(n_split + 1)
                        edges(j, k)
                        keep_clock(IDLE_PRODUCTS_POOLED, acc[:, 0, 1, 1])
                        hidden_sums(n_split + 1, 0)

            for_samples(pe, sample)


PARAM_DMAS = 1 + 3 * (2 * S * R + 2)
CHAIN = 63


def kernel(**inputs):
    import concourse.bacc as bacc
    from concourse.bass_utils import run_bass_kernel_spmd

    def lay(a):
        return np.ascontiguousarray(a)

    xs = np.asarray(inputs["x"]).reshape(B, HV, CH, G, R, WS, S).transpose(0, 6, 2, 4, 1, 3, 5)
    arrays = {"x": lay(xs).reshape(B, P, HV, G, WS)}
    for n, name in enumerate(("L0", "L2", "L3")):
        for part in ("w1", "b1", "w2", "b2"):
            arrays[f"{part}_{n}"] = lay(inputs[f"{name}_conv_{part}"])
    arrays["w_dense"] = lay(np.asarray(inputs["L1_conv_W"]).reshape(C, C, TAPS).transpose(1, 0, 2)).reshape(C, C * TAPS)
    arrays["consts"] = shape_constants()

    nc = bacc.Bacc("TRN2", target_bir_lowering=False, num_devices=1)
    aps = {name: nc.dram_tensor(name, a.shape, mybir.dt.from_np(a.dtype), kind="ExternalInput").ap()
           for name, a in arrays.items()}
    out = nc.dram_tensor("out", (B, P, HV, G, WS), F32, kind="ExternalOutput").ap()
    conv_preact_kernel(nc, aps["x"], *([aps[f"{part}_{n}"] for n in range(3)] for part in ("w1", "b1", "w2", "b2")),
                       aps["w_dense"], aps["consts"], out)
    r = run_bass_kernel_spmd(nc, [arrays], core_ids=[0])
    got = r.results[0]["out"].reshape(B, S, CH, R, HV, G, WS).transpose(0, 4, 2, 5, 3, 6, 1)
    return lay(got).reshape(B, C, H, W)
```
